# Optimizing a Trainium2 kernel written in Bass

```python
import numpy as np
import jax
import jax.numpy as jnp

def _softmax(x, axis=-1):
    return jax.nn.softmax(x, axis=axis)

def _gelu(x):
    return jax.nn.gelu(x, approximate=True)

def _silu(x):
    return jax.nn.silu(x)

def _sigmoid(x):
    return jax.nn.sigmoid(x)

def _layernorm(x, axis=-1, eps=1e-05):
    m = jnp.mean(x, axis=axis, keepdims=True)
    v = jnp.var(x, axis=axis, keepdims=True)
    return (x - m) / jnp.sqrt(v + eps)

def _scatter_add(tgt, idx, src, axis=0):
    return tgt.at[idx].add(src)

def _segment_sum(src, seg, n):
    return jax.ops.segment_sum(src, seg, n)
kernel_name = 'mk_dlrm_tower_d1_rec_r8_892607'

def setup_inputs(seed: int=0):
    np.random.seed(seed)
    _w = jnp.asarray

    def _rec_inputs():
        import jax
        import jax.numpy as jnp
        _tk = jax.random.key(seed)
        ids = jnp.stack([jax.random.randint(jax.random.fold_in(_tk, 200 + f), (512,), 0, v, jnp.int32) for f, v in enumerate([1000, 1250, 12500, 1250, 12500, 1000, 125000, 1000, 12500, 1250, 12500, 1000, 1250, 1250, 1250, 1250, 1250, 12500, 1000, 1250, 1000, 1250, 1000, 1000, 1000, 1000])], axis=1)
        tbl_0 = 0.05 * jax.random.normal(jax.random.fold_in(_tk, 500 + 0), (1000, 128), jnp.float32)
        tbl_1 = 0.05 * jax.random.normal(jax.random.fold_in(_tk, 500 + 1), (1250, 128), jnp.float32)
        tbl_2 = 0.05 * jax.random.normal(jax.random.fold_in(_tk, 500 + 2), (12500, 128), jnp.float32)
        tbl_3 = 0.05 * jax.random.normal(jax.random.fold_in(_tk, 500 + 3), (1250, 128), jnp.float32)
        tbl_4 = 0.05 * jax.random.normal(jax.random.fold_in(_tk, 500 + 4), (12500, 128), jnp.float32)
        tbl_5 = 0.05 * jax.random.normal(jax.random.fold_in(_tk, 500 + 5), (1000, 128), jnp.float32)
        tbl_6 = 0.05 * jax.random.normal(jax.random.fold_in(_tk, 500 + 6), (125000, 128), jnp.float32)
        tbl_7 = 0.05 * jax.random.normal(jax.random.fold_in(_tk, 500 + 7), (1000, 128), jnp.float32)
        tbl_8 = 0.05 * jax.random.normal(jax.random.fold_in(_tk, 500 + 8), (12500, 128), jnp.float32)
        tbl_9 = 0.05 * jax.random.normal(jax.random.fold_in(_tk, 500 + 9), (1250, 128), jnp.float32)
        tbl_10 = 0.05 * jax.random.normal(jax.random.fold_in(_tk, 500 + 10), (12500, 128), jnp.float32)
        tbl_11 = 0.05 * jax.random.normal(jax.random.fold_in(_tk, 500 + 11), (1000, 128), jnp.float32)
        tbl_12 = 0.05 * jax.random.normal(jax.random.fold_in(_tk, 500 + 12), (1250, 128), jnp.float32)
        tbl_13 = 0.05 * jax.random.normal(jax.random.fold_in(_tk, 500 + 13), (1250, 128), jnp.float32)
        tbl_14 = 0.05 * jax.random.normal(jax.random.fold_in(_tk, 500 + 14), (1250, 128), jnp.float32)
        tbl_15 = 0.05 * jax.random.normal(jax.random.fold_in(_tk, 500 + 15), (1250, 128), jnp.float32)
        tbl_16 = 0.05 * jax.random.normal(jax.random.fold_in(_tk, 500 + 16), (1250, 128), jnp.float32)
        tbl_17 = 0.05 * jax.random.normal(jax.random.fold_in(_tk, 500 + 17), (12500, 128), jnp.float32)
        tbl_18 = 0.05 * jax.random.normal(jax.random.fold_in(_tk, 500 + 18), (1000, 128), jnp.float32)
        tbl_19 = 0.05 * jax.random.normal(jax.random.fold_in(_tk, 500 + 19), (1250, 128), jnp.float32)
        tbl_20 = 0.05 * jax.random.normal(jax.random.fold_in(_tk, 500 + 20), (1000, 128), jnp.float32)
        tbl_21 = 0.05 * jax.random.normal(jax.random.fold_in(_tk, 500 + 21), (1250, 128), jnp.float32)
        tbl_22 = 0.05 * jax.random.normal(jax.random.fold_in(_tk, 500 + 22), (1000, 128), jnp.float32)
        tbl_23 = 0.05 * jax.random.normal(jax.random.fold_in(_tk, 500 + 23), (1000, 128), jnp.float32)
        tbl_24 = 0.05 * jax.random.normal(jax.random.fold_in(_tk, 500 + 24), (1000, 128), jnp.float32)
        tbl_25 = 0.05 * jax.random.normal(jax.random.fold_in(_tk, 500 + 25), (1000, 128), jnp.float32)
        _rk = jax.random.fold_in(_tk, 7)
        r_dense_features = -0.000520686 + 1.00062 * jax.random.normal(jax.random.fold_in(_rk, 101), (512, 128), jnp.float32)
        W_top1 = 0.0405887 * jax.random.normal(jax.random.fold_in(_tk, 801), (607, 512), jnp.float32)
        W_top2 = 0.0441942 * jax.random.normal(jax.random.fold_in(_tk, 802), (512, 256), jnp.float32)
        W_top3 = 0.0625 * jax.random.normal(jax.random.fold_in(_tk, 803), (256, 1), jnp.float32)
        b_top1 = jnp.zeros((512,), jnp.float32)
        b_top2 = jnp.zeros((256,), jnp.float32)
        return (r_dense_features, ids, tbl_0, tbl_1, tbl_2, tbl_3, tbl_4, tbl_5, tbl_6, tbl_7, tbl_8, tbl_9, tbl_10, tbl_11, tbl_12, tbl_13, tbl_14, tbl_15, tbl_16, tbl_17, tbl_18, tbl_19, tbl_20, tbl_21, tbl_22, tbl_23, tbl_24, tbl_25, W_top1, b_top1, W_top2, b_top2, W_top3)
    r_dense_features, ids, tbl_0, tbl_1, tbl_2, tbl_3, tbl_4, tbl_5, tbl_6, tbl_7, tbl_8, tbl_9, tbl_10, tbl_11, tbl_12, tbl_13, tbl_14, tbl_15, tbl_16, tbl_17, tbl_18, tbl_19, tbl_20, tbl_21, tbl_22, tbl_23, tbl_24, tbl_25, W_top1, b_top1, W_top2, b_top2, W_top3 = _rec_inputs()

    def _L0_rec_setup():
        import jax, jax.numpy as jnp
        import numpy as np
        NUM_SPARSE = 26
        EMBED_DIM = 128
        BATCH = 2048
        key = jax.random.key(seed)
        k1, k2 = jax.random.split(key)
        dense_features = jax.random.normal(k1, (BATCH, EMBED_DIM), dtype=jnp.float32)
        sparse_features = jax.random.normal(k2, (BATCH, NUM_SPARSE, EMBED_DIM), dtype=jnp.float32)
        return {'dense_features': dense_features, 'sparse_features': sparse_features}
    _L0_rec_all = _L0_rec_setup()
    _L0_rec_in = {k: v for k, v in _L0_rec_all.items() if k in ()}
    del _L0_rec_all
    return {'r_dense_features': r_dense_features, 'ids': ids, 'tbl_0': tbl_0, 'tbl_1': tbl_1, 'tbl_2': tbl_2, 'tbl_3': tbl_3, 'tbl_4': tbl_4, 'tbl_5': tbl_5, 'tbl_6': tbl_6, 'tbl_7': tbl_7, 'tbl_8': tbl_8, 'tbl_9': tbl_9, 'tbl_10': tbl_10, 'tbl_11': tbl_11, 'tbl_12': tbl_12, 'tbl_13': tbl_13, 'tbl_14': tbl_14, 'tbl_15': tbl_15, 'tbl_16': tbl_16, 'tbl_17': tbl_17, 'tbl_18': tbl_18, 'tbl_19': tbl_19, 'tbl_20': tbl_20, 'tbl_21': tbl_21, 'tbl_22': tbl_22, 'tbl_23': tbl_23, 'tbl_24': tbl_24, 'tbl_25': tbl_25, 'W_top1': W_top1, 'b_top1': b_top1, 'W_top2': W_top2, 'b_top2': b_top2, 'W_top3': W_top3}

def reference(r_dense_features, ids, tbl_0, tbl_1, tbl_2, tbl_3, tbl_4, tbl_5, tbl_6, tbl_7, tbl_8, tbl_9, tbl_10, tbl_11, tbl_12, tbl_13, tbl_14, tbl_15, tbl_16, tbl_17, tbl_18, tbl_19, tbl_20, tbl_21, tbl_22, tbl_23, tbl_24, tbl_25, W_top1, b_top1, W_top2, b_top2, W_top3):
    import jax
    import jax.numpy as jnp

    def _L0_rec_ref(dense_features, sparse_features):
        import jax, jax.numpy as jnp
        import numpy as np
        NUM_SPARSE = 26
        EMBED_DIM = 128
        BATCH = 2048
        F = NUM_SPARSE + 1
        combined = jnp.concatenate([dense_features[:, None, :], sparse_features], axis=1)
        interactions = jnp.einsum('bfd,bgd->bfg', combined, combined)
        iu, ju = jnp.triu_indices(F, k=1)
        interactions_flat = interactions[:, iu, ju]
        return jnp.concatenate([dense_features, interactions_flat], axis=1)
    e = jnp.stack([tbl_0[ids[:, 0]], tbl_1[ids[:, 1]], tbl_2[ids[:, 2]], tbl_3[ids[:, 3]], tbl_4[ids[:, 4]], tbl_5[ids[:, 5]], tbl_6[ids[:, 6]], tbl_7[ids[:, 7]], tbl_8[ids[:, 8]], tbl_9[ids[:, 9]], tbl_10[ids[:, 10]], tbl_11[ids[:, 11]], tbl_12[ids[:, 12]], tbl_13[ids[:, 13]], tbl_14[ids[:, 14]], tbl_15[ids[:, 15]], tbl_16[ids[:, 16]], tbl_17[ids[:, 17]], tbl_18[ids[:, 18]], tbl_19[ids[:, 19]], tbl_20[ids[:, 20]], tbl_21[ids[:, 21]], tbl_22[ids[:, 22]], tbl_23[ids[:, 23]], tbl_24[ids[:, 24]], tbl_25[ids[:, 25]]], axis=1)
    z = _L0_rec_ref(r_dense_features, e)
    z = z.reshape(z.shape[0], -1)
    h = jnp.concatenate([z, r_dense_features], axis=1)
    h = jnp.maximum(h @ W_top1 + b_top1, 0.0)
    h = jnp.maximum(h @ W_top2 + b_top2, 0.0)
    y = h @ W_top3
    return y

_drawn_inputs = setup_inputs


def setup_inputs(seed=0):
    import zlib

    import numpy as np

    out = dict(_drawn_inputs(seed))
    spreads = {'b_top1': (0.0, 0.1), 'b_top2': (0.0, 0.1)}
    factors = {}
    for name, (base, spread) in spreads.items():
        noise = np.random.default_rng([zlib.crc32(name.encode()), seed]).standard_normal(out[name].shape)
        drawn = base * np.exp(spread * noise) if base else spread * noise
        out[name] = jnp.asarray(drawn.astype(out[name].dtype))
    for name, factor in factors.items():
        out[name] = (out[name] * factor).astype(out[name].dtype)
    return out
```

```python
import concourse.bass as bass
from concourse import mybir
from contextlib import ExitStack

fp32 = mybir.dt.float32
fp32r = mybir.dt.float32r
int32 = mybir.dt.int32
ALU = mybir.AluOpType
ACT = mybir.ActivationFunctionType

P = 128
D = 128
TABLES = 26
F = TABLES + 1
TILES = 4
BATCH = TILES * P
ONE_HOT = [18, 20, 22, 23, 24, 25, 0]
ROWS = 1000
CH = 8
CD = CH - 1
RP = ROWS // CH
GATHER = [i for i in range(TABLES) if i not in ONE_HOT]
NG = len(GATHER)
GROUPS = [(2, 1, 4), (6, 1, 4), (10, 1, 4), (14, 1, 4), (18, 2, 3)]
GROUP_AT = [sum(n for _, _, n in GROUPS[:g]) for g in range(len(GROUPS))]
assert [f + s * i for f, s, n in GROUPS for i in range(n)] == [i + 1 for i in GATHER]
Q = 32
SPG = 4
GB = 7
GROUPS_PER_ROUND = 8
ROUNDS = P // (SPG * GROUPS_PER_ROUND)
ROW_BUFS = 3
AFTER = [(0, 1, 0, 1, 1), (0, 1, 1, 2, 1), (0, 1, 1, 2, 1), (0,) * 5]
N1, N2 = 512, 256
C1, C2 = N1 // P, N2 // P
PAIRS = F * (F - 1) // 2
PAIR_LOADS = sum((f % GB > 0) + (-(-f // GB) < SPG) for f in range(F - 1))


def pair_row(f, g):
    return D + f * F - f * (f + 1) // 2 + g - f - 1


def load_pairs(sp, f, w_pairs, w_top1, loaded):
    k, g0 = divmod(f, GB)
    loads = 0
    if g0:
        n = min(GB, F - 1 - GB * k) - g0
        r = pair_row(f, f + 1)
        sp.dma_start(w_pairs[Q * k + f:Q * k + f + 1, g0:g0 + n, :],
                     w_top1[r:r + n, :].rearrange("(o g) n -> o g n", o=1)).then_inc(loaded, 16)
        k += 1
        loads += 1
    if k < SPG:
        r = pair_row(f, 1 + GB * k)
        sp.dma_start(w_pairs[Q * k + f:P:Q, :, :],
                     w_top1[r:r + GB * (SPG - k), :].rearrange("(k g) n -> k g n", g=GB)).then_inc(loaded, 16)
        loads += 1
    return loads


def dlrm_tower(nc, A, out):
    ctx = ExitStack()
    with ctx:
        def sb(name, shape, dt=fp32):
            return ctx.enter_context(nc.sbuf_tensor(name, shape, dt))

        def sem(name):
            return ctx.enter_context(nc.semaphore(name))

        ids = sb("ids_i", [P, TILES * TABLES], int32)
        ids_f = sb("ids_f", [P, TILES * TABLES])
        ids_T = sb("ids_T", [TABLES, BATCH], fp32r)
        ident = sb("ident", [P, P])
        ident_r = sb("ident_r", [TABLES, TABLES], fp32r)
        row_of = sb("row_of", [P, CH])
        zero = sb("zero", [P, 1])
        one = sb("one", [P, 1])
        minus_row = sb("minus_row", [P, 1])
        far = sb("far", [RP, BATCH])
        dense = sb("dense", [P, TILES, D])
        dense_T = sb("dense_T", [D, TILES, P])
        rows = sb("rows", [P, NG, ROW_BUFS, D])
        feat = sb("feat", [D, TILES, P, Q])
        RAWS, SPLITS = 3, 2
        table = sb("table", [RP, RAWS, CH * D])
        table_hi = sb("table_hi", [RP, SPLITS, CH * D], fp32r)
        table_lo = sb("table_lo", [RP, SPLITS, CH * D], fp32r)
        ids_all = sb("ids_all", [P, SPLITS, BATCH])
        one_hot = sb("one_hot", [RP, SPLITS, CH, BATCH], fp32r)
        pairs = sb("pairs", [P, GB, TILES, SPG, P // SPG])
        w_pairs = sb("w_pairs", [P, GB, N1])
        w_dense = sb("w_dense", [P, 2, N1])
        w2 = sb("w2", [P, C1, N2])
        rows8 = sb("rows8", [C1 + 2 * C2, P])
        cols8 = sb("cols8", [P, C1 + 2 * C2])
        h1 = sb("h1", [P, C1, P])
        h2 = sb("h2", [P, C2, P])
        y = sb("y", [1, BATCH])

        ps_gram = ctx.enter_context(nc.psum_tensor("ps_gram", [P, 2, GROUPS_PER_ROUND, P], fp32))
        ps_x = [ctx.enter_context(nc.psum_tensor(f"ps_x{b}", [P, 512], fp32)) for b in range(2)]
        ps_l = [ctx.enter_context(nc.psum_tensor(f"ps_l{b}", [P, 512], fp32)) for b in range(2)]

        s_ids = sem("s_ids")
        s_small = sem("s_small")
        s_dense = sem("s_dense")
        s_w1 = sem("s_w1")
        s_wd = sem("s_wd")
        s_w2 = sem("s_w2")
        s_raw = [sem(f"s_raw{b}") for b in range(RAWS)]
        s_rows = [[sem(f"s_rows{t}_{g}") for g in range(len(GROUPS))] for t in range(TILES)]
        s_out = sem("s_out")
        s_memz = sem("s_memz")
        s_ident = sem("s_ident")
        s_zero = sem("s_zero")
        s_pad = sem("s_pad")
        s_idsf = sem("s_idsf")
        s_set = sem("s_set")
        s_idsT = sem("s_idsT")
        s_cols = sem("s_cols")
        s_bc = sem("s_bc")
        s_hi = sem("s_hi")
        s_lo = sem("s_lo")
        s_oh = sem("s_oh")
        s_far = sem("s_far")
        s_oh_act = sem("s_oh_act")
        s_consts = sem("s_consts")
        s_x = sem("s_x")
        s_xfree = [sem(f"s_xfree{b}") for b in range(2)]
        s_early = sem("s_early")
        s_early_out = sem("s_early_out")
        s_wds = sem("s_wds")
        s_gram = sem("s_gram")
        s_pk_act = sem("s_pk_act")
        s_pk_dve = sem("s_pk_dve")
        s_l = [sem(f"s_l{b}") for b in range(2)]
        s_lfree = [sem(f"s_lfree{b}") for b in range(2)]

        order = [("rows", t, g) for t in range(TILES) for g in range(len(GROUPS))]
        early = order[:len(ONE_HOT)]
        uses = [("dense",)] + [("look", i) for i in range(len(ONE_HOT))] + order[len(early):]
        use_of = {u: n for n, u in enumerate(uses)}

        def bank_of(use):
            return use_of[use] % 2

        def wait_bank(eng, use):
            n = use_of[use]
            if n >= 2:
                eng.wait_ge(s_xfree[n % 2], n // 2)

        def wait_feat(eng, t):
            if t == 0:
                eng.wait_ge(s_early_out, len(early))
            n = use_of.get(("rows", t, len(GROUPS) - 1), use_of[("look", len(ONE_HOT) - 1)])
            eng.wait_ge(s_xfree[n % 2], n // 2 + 1)
            eng.wait_ge(s_xfree[1 - n % 2], (n + 1) // 2)

        def rows_bank(u):
            if u in early:
                n = early.index(u)
                return ps_gram[:, n % 2, 0:4, :].rearrange("d f p -> d (f p)"), s_early, s_early_out, n
            return ps_x[bank_of(u)][:, :], s_x, s_xfree[bank_of(u)], use_of[u]

        BC = [len(range(b, len(ONE_HOT), 2)) for b in range(2)]

        def l_done(b, t, layer):
            return t * (3 - b) + layer

        def l_before(b, t, layer):
            return BC[b] + l_done(b, t, layer) - 1

        def feat_fields(t, f, step, n):
            return feat[:, t, :, f:f + step * (n - 1) + 1:step].rearrange("d p f -> d f p")

        block = ctx.enter_context(nc.Block())

        @block.sync
        def _(sp):
            def load_table(i):
                sp.dma_start(table[:, i % RAWS, :], A[f"tbl_{ONE_HOT[i]}"].rearrange("(p c) d -> p (c d)", c=CH))\
                  .then_inc(s_raw[i % RAWS], 16)

            sp.dma_start(ids[:, :], A["ids"].rearrange("(p t) f -> p (t f)", t=TILES)).then_inc(s_ids, 16)
            load_table(0)
            sp.dma_start(dense[:, :, :], A["r_dense_features"].rearrange("(p t) d -> p t d", t=TILES))\
              .then_inc(s_dense, 16)
            sp.dma_start(rows8[0:C1, :], A["b_top1"].rearrange("(c p) -> c p", p=P)).then_inc(s_small, 16)
            sp.dma_start(rows8[C1:C1 + C2, :], A["b_top2"].rearrange("(c p) -> c p", p=P)).then_inc(s_small, 16)
            sp.dma_start(rows8[C1 + C2:C1 + 2 * C2, :], A["W_top3"].rearrange("(c p) o -> c (p o)", p=P))\
              .then_inc(s_small, 16)
            for i in range(1, len(ONE_HOT)):
                if i >= RAWS:
                    sp.wait_ge(s_lo, i - RAWS + 1)
                load_table(i)
                if i == RAWS - 1:
                    for half, r0 in enumerate((0, D + PAIRS)):
                        sp.dma_start(w_dense[:, half, :], A["W_top1"][r0:r0 + D, :]).then_inc(s_wd, 16)
                    sp.wait_ge(s_zero, 2)
                if i >= RAWS - 1:
                    n = len(ONE_HOT) - RAWS + 1
                    for f in range(i - RAWS + 1, F - 1, n):
                        load_pairs(sp, f, w_pairs, A["W_top1"], s_w1)
            sp.dma_start(w2[:, :, :], A["W_top2"].rearrange("(c p) n -> p c n", p=P)).then_inc(s_w2, 16)
            sp.wait_ge(s_lfree[0], l_before(0, TILES - 1, 3) + 1)
            sp.dma_start(out.rearrange("(a b) c -> a (b c)", a=1), y[:, :]).then_inc(s_out, 16)
            sp.wait_ge(s_out, 16)

        @block.gpsimd
        def _(pool):
            pool.memset(ident[:, :], 0.0).then_inc(s_memz, 1)
            pool.wait_ge(s_memz, 1)
            pool.affine_select(out=ident[:, :], in_=ident[:, :], compare_op=ALU.not_equal, fill=1.0,
                               base=0, pattern=[[-1, P]], channel_multiplier=1).then_inc(s_ident, 1)
            pool.iota(row_of[:, :], pattern=[[1, CH]], base=0, channel_multiplier=CH,
                      allow_small_or_imprecise_dtypes=True).then_inc(s_ident, 1)
            pool.wait_ge(s_ids, 16)
            for t in range(TILES):
                if t >= ROW_BUFS:
                    _, full, _, use = rows_bank(("rows", t - ROW_BUFS, len(GROUPS) - 1))
                    pool.wait_ge(full, use + 1)
                for g, (_, _, n) in enumerate(GROUPS):
                    for at in range(GROUP_AT[g], GROUP_AT[g] + n):
                        col = t * TABLES + GATHER[at]
                        pool.indirect_dma_start(
                            rows[:, at, t % ROW_BUFS, :], None, A[f"tbl_{GATHER[at]}"],
                            bass.IndirectOffsetOnAxis(ap=ids[:, col:col + 1], axis=0),
                        ).then_inc(s_rows[t][g], 16)

        after, at = {}, len(early)
        for t in range(TILES):
            for step in range(ROUNDS + 1):
                n = min(AFTER[t][step], len(order) - at)
                after[t, step] = order[at:at + n]
                at += n
        assert at == len(order)

        def rows_out(eng, copy, groups):
            for u in groups:
                if (order.index(u) % 2 == 0) == (eng is nc.vector):
                    evac_rows(eng, copy, *u[1:])

        def evac_rows(eng, copy, t, g):
            f, step, n = GROUPS[g]
            bank, full, free, use = rows_bank(("rows", t, g))
            eng.wait_ge(full, use + 1)
            copy(feat_fields(t, f, step, n), bank[:, 0:n * P].rearrange("d (f p) -> d f p", p=P)).then_inc(free, 1)

        def pack(eng, copy, t, h, quadrants, done):
            eng.wait_ge(s_gram, ROUNDS * t + h + 1)
            for j in quadrants:
                for k in range(SPG):
                    n = min(GB, F - 1 - GB * k)
                    m = GROUPS_PER_ROUND
                    at = (F - 1) * j + GB * k
                    src = ps_gram[Q * j:Q * j + Q, h % 2, :, at:at + n]
                    last = copy(pairs[Q * k:Q * k + Q, 0:n, t, j, m * h:m * h + m],
                                src.rearrange("f m g -> f g m"))
            last.then_inc(done, 1)

        @block.scalar
        def _(act):
            def copy(dst, src):
                return act.activation(dst, src, ACT.Copy)

            def zero_pads(t):
                act.activation(feat[:, t:t + 2, :, F:Q].rearrange("d t p f -> d (t p) f"),
                               zero[:, :].unsqueeze(2).to_broadcast([D, 2 * P, Q - F]), ACT.Copy)\
                   .then_inc(s_pad, 1)

            act.wait_ge(s_zero, 1)
            zero_pads(0)
            act.wait_ge(s_ident, 1)
            copy(ident_r[:, :], ident[0:TABLES, 0:TABLES]).then_inc(s_idsT, 1)
            act.wait_ge(s_set, 1)
            copy(ids_T[:, :], ps_gram[0:TABLES, 0, 0:TILES, :]).then_inc(s_idsT, 1)

            def ids_out(i):
                act.wait_ge(s_bc, i + 1)
                if i >= SPLITS:
                    act.wait_ge(s_oh, CD * (i - SPLITS + 1))
                copy(ids_all[:, i % SPLITS, :], ps_l[i % 2][:, :]).then_inc(s_lfree[i % 2], 1)

            def split_hi(i):
                act.wait_ge(s_raw[i % RAWS], 16 * (i // RAWS + 1))
                if i >= SPLITS:
                    act.wait_ge(s_x, use_of[("look", i - SPLITS)] + 1)
                copy(table_hi[:, i % SPLITS, :], table[:, i % RAWS, :]).then_inc(s_hi, 1)

            def compare_ids(i):
                b = i % SPLITS
                if i == 0:
                    act.wait_ge(s_consts, 1)
                if i >= SPLITS:
                    act.wait_ge(s_x, use_of[("look", i - SPLITS)] + 1)
                act.wait_ge(s_lfree[i % 2], i // 2 + 1)
                if i:
                    act.wait_ge(s_oh_act, i)
                act.activation(far[:, :], ids_all[0:RP, b, :], ACT.Abs, bias=minus_row[0:RP, :])\
                   .then_inc(s_far, 1)
                act.wait_ge(s_far, i + 1)
                act.activation(one_hot[:, b, CH - 1, :], far[:, :], ACT.Relu, bias=one[0:RP, :], scale=-1.0)\
                   .then_inc(s_oh_act, 1)

            def looked_out(i):
                use = ("look", i)
                act.wait_ge(s_x, use_of[use] + 1)
                dst = feat[:, :, :, ONE_HOT[i] + 1]
                copy(dst, ps_x[bank_of(use)][:, :].rearrange("d (t p) -> d t p", t=TILES))\
                    .then_inc(s_xfree[bank_of(use)], 1)

            ids_out(0)
            split_hi(0)
            ids_out(1)
            compare_ids(0)
            split_hi(1)
            act.wait_ge(s_x, 1)
            src = ps_x[0][:, :].rearrange("d (t p) -> d t p", t=TILES)
            for t in range(TILES):
                copy(dense_T[:, t, :].rearrange("d (j m) -> d j m", j=SPG),
                     src[:, t, :].rearrange("d (m j) -> d j m", j=SPG))
            copy(feat[:, :, :, 0], src).then_inc(s_xfree[0], 1)
            act.wait_ge(s_set, 2)
            copy(cols8[:, :], ps_gram[:, 1, 0, 0:C1 + 2 * C2]).then_inc(s_cols, 1)
            compare_ids(1)
            for i in range(len(ONE_HOT)):
                if i + 2 < len(ONE_HOT):
                    ids_out(i + 2)
                looked_out(i)
                if i + 2 < len(ONE_HOT):
                    compare_ids(i + 2)
                    split_hi(i + 2)
                evac_rows(act, copy, *early[i][1:])
                if i == 0:
                    zero_pads(2)
            act.wait_ge(s_cols, 1)
            def layer2_out(t):
                act.wait_ge(s_l[1], l_done(1, t, 2))
                act.activation(h2[:, 1, :], ps_l[1][:, 0:P], ACT.Relu,
                               bias=cols8[:, C1 + 1:C1 + 2]).then_inc(s_lfree[1], 1)

            for t in range(TILES):
                for h in range(ROUNDS):
                    pack(act, copy, t, h, (2, 3), s_pk_act)
                    if t and h == 1:
                        layer2_out(t - 1)
                    rows_out(act, copy, after[t, h])
                rows_out(act, copy, after[t, ROUNDS])
                act.wait_ge(s_l[1], l_done(1, t, 1))
                for c in range(2):
                    last = act.activation(h1[:, 2 + c, :], ps_l[1][:, c * P:c * P + P], ACT.Relu,
                                          bias=cols8[:, 2 + c:3 + c])
                last.then_inc(s_lfree[1], 1)
            layer2_out(TILES - 1)

        @block.vector
        def _(dve):
            def copy(dst, src):
                return dve.tensor_copy(dst, src)

            dve.memset(zero[:, :], 0.0).then_inc(s_zero, 1)
            half = GB // 2 + 1
            dve.memset(w_pairs[:, 0:half, :], 0.0)
            dve.wait_ge(s_ids, 16)
            copy(ids_f[:, :], ids[:, :]).then_inc(s_idsf, 1)
            dve.memset(w_pairs[:, half:GB, :], 0.0).then_inc(s_zero, 1)

            def split_lo(i):
                b = i % SPLITS
                dve.wait_ge(s_hi, i + 1)
                if i >= SPLITS:
                    dve.wait_ge(s_x, use_of[("look", i - SPLITS)] + 1)
                dve.tensor_tensor(table_lo[:, b, :], table[:, i % RAWS, :], table_hi[:, b, :].bitcast(fp32),
                                  ALU.subtract).then_inc(s_lo, 1)

            def compare_ids(i):
                b = i % SPLITS
                dve.wait_ge(s_lfree[i % 2], i // 2 + 1)
                if i >= SPLITS:
                    dve.wait_ge(s_x, use_of[("look", i - SPLITS)] + 1)
                for c in range(CD):
                    dve.tensor_scalar(one_hot[:, b, c, :], ids_all[0:RP, b, :], row_of[0:RP, c:c + 1], None,
                                      ALU.is_equal).then_inc(s_oh, 1)

            dve.memset(one[:, :], 1.0)
            dve.wait_ge(s_ident, 2)
            dve.tensor_scalar(minus_row[:, :], row_of[:, CH - 1:CH], -1.0, None, ALU.mult).then_inc(s_consts, 1)
            for i in range(len(ONE_HOT)):
                compare_ids(i)
                split_lo(i)
            dve.wait_ge(s_wd, 32)
            dve.tensor_tensor(w_dense[:, 0, :], w_dense[:, 0, :], w_dense[:, 1, :], ALU.add).then_inc(s_wds, 1)
            dve.wait_ge(s_cols, 1)

            def relu(dst, src, bias):
                return dve.tensor_scalar(dst, src, bias, 0.0, ALU.add, ALU.max)

            def layer2_out(t):
                dve.wait_ge(s_l[0], l_done(0, t, 2))
                relu(h2[:, 0, :], ps_l[0][:, 0:P], cols8[:, C1:C1 + 1]).then_inc(s_lfree[0], 1)

            def layer3_out(t):
                dve.wait_ge(s_l[0], l_done(0, t, 3))
                dst = y[:, :].rearrange("o (m j t) -> o t j m", j=SPG, t=TILES)[:, t, :, :]
                copy(dst, ps_l[0][0:1, 0:P].rearrange("o (j m) -> o j m", j=SPG)).then_inc(s_lfree[0], 1)

            for t in range(TILES):
                for h in range(ROUNDS):
                    pack(dve, copy, t, h, (0, 1), s_pk_dve)
                    if t and h == 1:
                        layer2_out(t - 1)
                    if t and h == ROUNDS - 1:
                        layer3_out(t - 1)
                    rows_out(dve, copy, after[t, h])
                rows_out(dve, copy, after[t, ROUNDS])
                dve.wait_ge(s_l[0], l_done(0, t, 1))
                for c in range(2):
                    last = relu(h1[:, c, :], ps_l[0][:, c * P:c * P + P], cols8[:, c:c + 1])
                last.then_inc(s_lfree[0], 1)
            layer2_out(TILES - 1)
            layer3_out(TILES - 1)

        @block.tensor
        def _(pe):
            def keep_warm(n):
                for _ in range(n):
                    pe.transpose(ps_l[1][:, 0:P], ident[:, :], ident[:, :])

            pe.wait_ge(s_ident, 1)
            keep_warm(8)
            pe.wait_ge(s_idsf, 1)
            for t in range(TILES):
                last = pe.transpose(ps_gram[0:TABLES, 0, t, :], ids_f[:, t * TABLES:t * TABLES + TABLES], ident[:, :])
            last.then_inc(s_set, 1)
            def broadcast_ids(i):
                if i == 0:
                    pe.wait_ge(s_idsT, 2)
                if i >= 2:
                    pe.wait_ge(s_lfree[i % 2], i // 2)
                tb = ONE_HOT[i]
                pe.matmul(ps_l[i % 2][:, :], ident_r[:, tb:tb + 1].to_broadcast([TABLES, P]), ids_T[:, :],
                          start=True, stop=True).then_inc(s_bc, 1)

            def lookup(i):
                b = i % SPLITS
                use = ("look", i)
                wait_bank(pe, use)
                pe.wait_ge(s_hi, i + 1)
                steps = [(c, part) for part in (table_hi, table_lo) for c in range(CH)]
                for n, (c, part) in enumerate(steps):
                    if part is table_hi and c < CD:
                        pe.wait_ge(s_oh, CD * i + c + 1)
                    elif part is table_hi:
                        pe.wait_ge(s_oh_act, i + 1)
                    elif c == 0:
                        pe.wait_ge(s_lo, i + 1)
                    last = pe.matmul(ps_x[bank_of(use)][:, :], part[:, b, c * D:c * D + D],
                                     one_hot[:, b, c, :], start=(n == 0), stop=(n == len(steps) - 1))
                last.then_inc(s_x, 1)

            def transpose_rows(t, g):
                u = ("rows", t, g)
                bank, full, free, use = rows_bank(u)
                if u not in early:
                    wait_bank(pe, u)
                elif use >= 2:
                    pe.wait_ge(free, use - 1)
                elif use:
                    pe.wait_ge(s_cols, 1)
                pe.wait_ge(s_rows[t][g], 16 * GROUPS[g][2])
                for n in range(GROUPS[g][2]):
                    last = pe.transpose(bank[:, n * P:n * P + P],
                                        rows[:, GROUP_AT[g] + n, t % ROW_BUFS, :], ident[:, :])
                last.then_inc(full, 1)

            def grams(t, h):
                r = ROUNDS * t + h
                if h == 0:
                    wait_feat(pe, t)
                    if t % 2 == 0:
                        pe.wait_ge(s_pad, t // 2 + 1)
                if r >= 2:
                    pe.wait_ge(s_pk_act, r - 1)
                    pe.wait_ge(s_pk_dve, r - 1)
                for m in range(GROUPS_PER_ROUND):
                    at = (h * GROUPS_PER_ROUND + m) * SPG
                    samples = feat[:, t, at:at + SPG, :]
                    last = pe.matmul(ps_gram[:, h % 2, m, 0:SPG * (F - 1)], samples.rearrange("d s f -> d (s f)"),
                                     samples[:, :, 1:F], start=True, stop=True)
                last.then_inc(s_gram, 1)

            def layer1(t):
                if t == 0:
                    pe.wait_ge(s_wds, 1)
                    pe.wait_ge(s_w1, 16 * PAIR_LOADS)
                def column(c):
                    return ps_l[c // 2][:, (c % 2) * P:(c % 2) * P + P]

                def from_dense(c):
                    pe.matmul(column(c), w_dense[:, 0, c * P:c * P + P], dense_T[:, t, :], start=True, stop=False)

                def from_pairs(c):
                    for g in range(GB):
                        kp = P if GB * (SPG - 1) + g < F - 1 else P - Q
                        last = pe.matmul(column(c), w_pairs[0:kp, g, c * P:c * P + P],
                                         pairs[0:kp, g, t, :, :].rearrange("p j m -> p (j m)"),
                                         start=False, stop=(g == GB - 1))
                    return last

                for b in range(2):
                    pe.wait_ge(s_lfree[b], l_before(b, t, 1))
                    from_dense(2 * b)
                pe.wait_ge(s_pk_act, ROUNDS * (t + 1))
                pe.wait_ge(s_pk_dve, ROUNDS * (t + 1))
                for b in range(2):
                    from_pairs(2 * b)
                for u in after[t, ROUNDS]:
                    transpose_rows(*u[1:])
                for b in range(2):
                    from_dense(2 * b + 1)
                    from_pairs(2 * b + 1).then_inc(s_l[b], 1)

            def layer2(t):
                if t == 0:
                    pe.wait_ge(s_w2, 16)
                for m in range(C2):
                    for c in range(C1):
                        if m == 0 and c % 2 == 0:
                            b = c // 2
                            pe.wait_ge(s_lfree[b], l_before(b, t, 2))
                        last = pe.matmul(ps_l[m][:, 0:P], w2[:, c, m * P:m * P + P], h1[:, c, :],
                                         start=(c == 0), stop=(c == C1 - 1))
                    last.then_inc(s_l[m], 1)

            def layer3(t):
                pe.wait_ge(s_lfree[0], l_before(0, t, 3))
                pe.wait_ge(s_lfree[1], l_before(1, t, 3))
                for m in range(C2):
                    last = pe.matmul(ps_l[0][0:1, 0:P], cols8[:, C1 + C2 + m:C1 + C2 + m + 1],
                                     h2[:, m, :], start=(m == 0), stop=(m == C2 - 1))
                last.then_inc(s_l[0], 1)

            keep_warm(2)
            broadcast_ids(0)
            pe.wait_ge(s_dense, 16)
            for t in range(TILES):
                last = pe.transpose(ps_x[0][:, t * P:t * P + P], dense[:, t, :], ident[:, :])
            last.then_inc(s_x, 1)
            broadcast_ids(1)
            pe.wait_ge(s_small, 48)
            pe.transpose(ps_gram[:, 1, 0, 0:C1 + 2 * C2], rows8[:, :], ident[0:C1 + 2 * C2, 0:C1 + 2 * C2])\
              .then_inc(s_set, 1)
            for i in range(len(ONE_HOT)):
                if i + 2 < len(ONE_HOT):
                    broadcast_ids(i + 2)
                lookup(i)
                transpose_rows(*early[i][1:])
            for t in range(TILES):
                for h in range(ROUNDS):
                    grams(t, h)
                    if t and h == 1:
                        layer2(t - 1)
                    if t and h == ROUNDS - 1:
                        layer3(t - 1)
                    for u in after[t, h]:
                        transpose_rows(*u[1:])
                layer1(t)
            layer2(TILES - 1)
            layer3(TILES - 1)


_IN = (["r_dense_features", "ids"] + [f"tbl_{i}" for i in range(TABLES)]
       + ["W_top1", "b_top1", "W_top2", "b_top2", "W_top3"])


def kernel(**inputs):
    import numpy as _np
    import concourse.bacc as _bacc
    from concourse import mybir as _mybir
    from concourse.bass_utils import run_bass_kernel_spmd as _run

    nc = _bacc.Bacc("TRN2", target_bir_lowering=False, num_devices=1)
    arrays, args = {}, {}
    for name in _IN:
        a = _np.ascontiguousarray(inputs[name])
        arrays[f"in_{name}_dram"] = a
        args[name] = nc.dram_tensor(f"in_{name}_dram", a.shape, _mybir.dt.from_np(a.dtype),
                                    kind="ExternalInput").ap()
    out = nc.dram_tensor("out_0_dram", (BATCH, 1), _mybir.dt.float32, kind="ExternalOutput").ap()
    dlrm_tower(nc, args, out)
    r = _run(nc, [arrays], core_ids=[0])
    return r.results[0]["out_0_dram"]
```

```python
import concourse.bass as bass
from concourse import mybir
from contextlib import ExitStack

fp32 = mybir.dt.float32
fp32r = mybir.dt.float32r
int32 = mybir.dt.int32
ALU = mybir.AluOpType
ACT = mybir.ActivationFunctionType

P = 128
D = 128
TABLES = 26
F = TABLES + 1
TILES = 4
BATCH = TILES * P
ONE_HOT = [18, 20, 22, 23, 24, 25, 0]
ROWS = 1000
CH = 8
CD = CH - 1
RP = ROWS // CH
GATHER = [i for i in range(TABLES) if i not in ONE_HOT]
NG = len(GATHER)
GROUPS = [(2, 1, 4), (6, 1, 4), (10, 1, 4), (14, 1, 4), (18, 2, 3)]
GROUP_AT = [sum(n for _, _, n in GROUPS[:g]) for g in range(len(GROUPS))]
assert [f + s * i for f, s, n in GROUPS for i in range(n)] == [i + 1 for i in GATHER]
Q = 32
SPG = 4
GB = 7
GROUPS_PER_ROUND = 8
ROUNDS = P // (SPG * GROUPS_PER_ROUND)
ROW_BUFS = 3
BETWEEN = [(1, 0, 0, 0, 2, 1, 0), (0, 0, 1, 1, 1, 1, 1), (0, 0, 1, 1, 1, 1, 1), (0,) * 7]
N1, N2 = 512, 256
C1, C2 = N1 // P, N2 // P
PAIRS = F * (F - 1) // 2
PAIR_LOADS = sum((f % GB > 0) + (-(-f // GB) < SPG) for f in range(F - 1))


def pair_row(f, g):
    return D + f * F - f * (f + 1) // 2 + g - f - 1


def load_pairs(sp, f, w_pairs, w_top1, loaded):
    k, g0 = divmod(f, GB)
    loads = 0
    if g0:
        n = min(GB, F - 1 - GB * k) - g0
        r = pair_row(f, f + 1)
        sp.dma_start(w_pairs[Q * k + f:Q * k + f + 1, g0:g0 + n, :],
                     w_top1[r:r + n, :].rearrange("(o g) n -> o g n", o=1)).then_inc(loaded, 16)
        k += 1
        loads += 1
    if k < SPG:
        r = pair_row(f, 1 + GB * k)
        sp.dma_start(w_pairs[Q * k + f:P:Q, :, :],
                     w_top1[r:r + GB * (SPG - k), :].rearrange("(k g) n -> k g n", g=GB)).then_inc(loaded, 16)
        loads += 1
    return loads


def dlrm_tower(nc, A, out):
    ctx = ExitStack()
    with ctx:
        def sb(name, shape, dt=fp32):
            return ctx.enter_context(nc.sbuf_tensor(name, shape, dt))

        def sem(name):
            return ctx.enter_context(nc.semaphore(name))

        ids = sb("ids_i", [P, TILES * TABLES], int32)
        ids_f = sb("ids_f", [P, TILES * TABLES])
        ids_T = sb("ids_T", [TABLES, BATCH], fp32r)
        ident = sb("ident", [P, P])
        ident_r = sb("ident_r", [TABLES, TABLES], fp32r)
        row_of = sb("row_of", [P, CH])
        zero = sb("zero", [P, 1])
        one = sb("one", [P, 1])
        minus_row = sb("minus_row", [P, 1])
        far = sb("far", [RP, BATCH])
        dense = sb("dense", [P, TILES, D])
        dense_T = sb("dense_T", [D, TILES, P])
        rows = sb("rows", [P, NG, ROW_BUFS, D])
        feat = sb("feat", [D, TILES, P, Q])
        RAWS, SPLITS = 3, 2
        HALF = CH * D // 2
        table = sb("table", [RP, RAWS, CH * D])
        table_hi = sb("table_hi", [RP, SPLITS, CH * D], fp32r)
        table_lo = sb("table_lo", [RP, SPLITS, CH * D], fp32r)
        ids_all = sb("ids_all", [P, SPLITS, BATCH])
        one_hot = sb("one_hot", [RP, SPLITS, CH, BATCH], fp32r)
        pairs = sb("pairs", [P, GB, TILES, SPG, P // SPG])
        w_pairs = sb("w_pairs", [P, GB, N1])
        w_dense = sb("w_dense", [P, 2, N1])
        w2 = sb("w2", [P, C1, N2])
        rows8 = sb("rows8", [C1 + 2 * C2, P])
        cols8 = sb("cols8", [P, C1 + 2 * C2])
        h1 = sb("h1", [P, C1, P])
        h2 = sb("h2", [P, C2, P])
        y = sb("y", [P, TILES])

        ps_gram = ctx.enter_context(nc.psum_tensor("ps_gram", [P, 2, GROUPS_PER_ROUND, P], fp32))
        ps_x = [ctx.enter_context(nc.psum_tensor(f"ps_x{b}", [P, 512], fp32)) for b in range(2)]
        ps_l = [ctx.enter_context(nc.psum_tensor(f"ps_l{b}", [P, 512], fp32)) for b in range(2)]

        s_ids = sem("s_ids")
        s_small = sem("s_small")
        s_dense = sem("s_dense")
        s_w1 = sem("s_w1")
        s_wd = sem("s_wd")
        s_w2 = sem("s_w2")
        s_first = sem("s_first")
        s_raw = [sem(f"s_raw{b}") for b in range(RAWS)]
        s_rows = [[sem(f"s_rows{t}_{g}") for g in range(len(GROUPS))] for t in range(TILES)]
        s_out = sem("s_out")
        s_memz = sem("s_memz")
        s_ident = sem("s_ident")
        s_zero = sem("s_zero")
        s_pad = sem("s_pad")
        s_idsf = sem("s_idsf")
        s_set = sem("s_set")
        s_idsT = sem("s_idsT")
        s_cols = sem("s_cols")
        s_bc = sem("s_bc")
        s_hi = sem("s_hi")
        s_lo = sem("s_lo")
        s_oh = sem("s_oh")
        s_far = sem("s_far")
        s_oh_act = sem("s_oh_act")
        s_consts = sem("s_consts")
        s_x = sem("s_x")
        s_xfree = [sem(f"s_xfree{b}") for b in range(2)]
        s_early = sem("s_early")
        s_early_out = sem("s_early_out")
        s_wds = sem("s_wds")
        s_gram = sem("s_gram")
        s_pk_act = sem("s_pk_act")
        s_pk_dve = sem("s_pk_dve")
        s_l = [sem(f"s_l{b}") for b in range(2)]
        s_tail = sem("s_tail")
        s_tail_out = sem("s_tail_out")
        s_lfree = [sem(f"s_lfree{b}") for b in range(2)]

        IN_LAYER1 = ROUNDS + 1
        order = [("rows", t, g) for t in range(TILES) for g in range(len(GROUPS))]
        early = order[:len(ONE_HOT) - 1]
        between, at = {}, len(early)
        uses = [("dense",)] + [("look", i) for i in range(len(ONE_HOT))]
        for t in range(TILES):
            for step in range(ROUNDS + 3):
                n = BETWEEN[t][step]
                between[t, step] = order[at:at + n]
                at += n
                if t and step == IN_LAYER1:
                    uses += [("out", t - 1)]
                uses += between[t, step]
        uses += [("out", TILES - 1)]
        assert at == len(order)
        use_of = {u: n for n, u in enumerate(uses)}

        def bank_of(use):
            return use_of[use] % 2

        def wait_bank(eng, use):
            n = use_of[use]
            if n >= 2:
                eng.wait_ge(s_xfree[n % 2], n // 2)

        def wait_feat(eng, t):
            if t < 2:
                eng.wait_ge(s_early_out, len([u for u in early if u[1] <= t]))
            n = use_of.get(("rows", t, len(GROUPS) - 1), use_of[("look", len(ONE_HOT) - 1)])
            eng.wait_ge(s_xfree[n % 2], n // 2 + 1)
            eng.wait_ge(s_xfree[1 - n % 2], (n + 1) // 2)

        def rows_bank(u):
            if u in early:
                n = early.index(u)
                return ps_gram[:, n % 2, 0:4, :].rearrange("d f p -> d (f p)"), s_early, s_early_out, n
            return ps_x[bank_of(u)][:, :], s_x, s_xfree[bank_of(u)], use_of[u]

        BC = [len(range(b, len(ONE_HOT), 2)) for b in range(2)]

        def l_done(t, layer):
            return 2 * t + layer

        def l_before(b, t, layer):
            return BC[b] + l_done(t, layer) - 1

        def layer1_column(t, c):
            if t == TILES - 1 and c == C1 - 1:
                return ps_gram[:, 0, 0, :]
            return ps_l[c // 2][:, (c % 2) * P:(c % 2) * P + P]

        def feat_fields(t, f, step, n):
            return feat[:, t, :, f:f + step * (n - 1) + 1:step].rearrange("d p f -> d f p")

        block = ctx.enter_context(nc.Block())

        @block.sync
        def _(sp):
            def load_table(i):
                sp.dma_start(table[:, i % RAWS, :], A[f"tbl_{ONE_HOT[i]}"].rearrange("(p c) d -> p (c d)", c=CH))\
                  .then_inc(s_raw[i % RAWS], 16)

            sp.dma_start(ids[:, :], A["ids"].rearrange("(p t) f -> p (t f)", t=TILES)).then_inc(s_ids, 16)
            for half, landed in ((0, s_first), (1, s_raw[0])):
                sp.dma_start(table[:, 0, half * HALF:half * HALF + HALF],
                             A[f"tbl_{ONE_HOT[0]}"].rearrange("(p c) d -> p (c d)", c=CH)
                             [:, half * HALF:half * HALF + HALF]).then_inc(landed, 16)
            sp.dma_start(dense[:, :, :], A["r_dense_features"].rearrange("(p t) d -> p t d", t=TILES))\
              .then_inc(s_dense, 16)
            sp.dma_start(rows8[0:C1, :], A["b_top1"].rearrange("(c p) -> c p", p=P)).then_inc(s_small, 16)
            sp.dma_start(rows8[C1:C1 + C2, :], A["b_top2"].rearrange("(c p) -> c p", p=P)).then_inc(s_small, 16)
            sp.dma_start(rows8[C1 + C2:C1 + 2 * C2, :], A["W_top3"].rearrange("(c p) o -> c (p o)", p=P))\
              .then_inc(s_small, 16)
            for i in range(1, len(ONE_HOT)):
                if i >= RAWS:
                    sp.wait_ge(s_lo, i - RAWS + 2)
                load_table(i)
                if i == RAWS - 1:
                    for half, r0 in enumerate((0, D + PAIRS)):
                        sp.dma_start(w_dense[:, half, :], A["W_top1"][r0:r0 + D, :]).then_inc(s_wd, 16)
                    sp.wait_ge(s_zero, 2)
                if i >= RAWS - 1:
                    n = 3
                    first = n * (i - RAWS + 1)
                    for f in range(first, first + n if i + 1 < len(ONE_HOT) else F - 1):
                        load_pairs(sp, f, w_pairs, A["W_top1"], s_w1)
            sp.dma_start(w2[:, :, :], A["W_top2"].rearrange("(c p) n -> p c n", p=P)).then_inc(s_w2, 16)
            for b in range(2):
                sp.wait_ge(s_xfree[b], len(range(b, len(uses), 2)))
            sp.dma_start(out.rearrange("(p t) c -> p (t c)", t=TILES), y[:, :]).then_inc(s_out, 16)
            sp.wait_ge(s_out, 16)

        @block.gpsimd
        def _(pool):
            pool.memset(ident[:, :], 0.0).then_inc(s_memz, 1)
            pool.wait_ge(s_memz, 1)
            pool.affine_select(out=ident[:, :], in_=ident[:, :], compare_op=ALU.not_equal, fill=1.0,
                               base=0, pattern=[[-1, P]], channel_multiplier=1).then_inc(s_ident, 1)
            pool.iota(row_of[:, :], pattern=[[1, CH]], base=0, channel_multiplier=CH,
                      allow_small_or_imprecise_dtypes=True).then_inc(s_ident, 1)
            pool.wait_ge(s_ids, 16)
            for t in range(TILES):
                if t >= ROW_BUFS:
                    _, full, _, use = rows_bank(("rows", t - ROW_BUFS, len(GROUPS) - 1))
                    pool.wait_ge(full, use + 1)
                for g, (_, _, n) in enumerate(GROUPS):
                    for at in range(GROUP_AT[g], GROUP_AT[g] + n):
                        col = t * TABLES + GATHER[at]
                        pool.indirect_dma_start(
                            rows[:, at, t % ROW_BUFS, :], None, A[f"tbl_{GATHER[at]}"],
                            bass.IndirectOffsetOnAxis(ap=ids[:, col:col + 1], axis=0),
                        ).then_inc(s_rows[t][g], 16)

        def read_by(u):
            return (nc.scalar, nc.vector)[bank_of(u)]

        def out_layer_out(eng, copy, t):
            u = ("out", t)
            if read_by(u) is eng:
                eng.wait_ge(s_x, use_of[u] + 1)
                copy(y[:, t:t + 1], ps_x[bank_of(u)][:, 0:1]).then_inc(s_xfree[bank_of(u)], 1)

        def in_order(op, dst, src, *args, **kw):
            return op(dst.rearrange("n (m j) -> n j m", j=SPG), src.rearrange("n (j m) -> n j m", j=SPG), *args, **kw)

        def rows_out(eng, copy, groups):
            for u in groups:
                if read_by(u) is eng:
                    evac_rows(eng, copy, *u[1:])

        def evac_rows(eng, copy, t, g):
            f, step, n = GROUPS[g]
            bank, full, free, use = rows_bank(("rows", t, g))
            eng.wait_ge(full, use + 1)
            copy(feat_fields(t, f, step, n), bank[:, 0:n * P].rearrange("d (f p) -> d f p", p=P)).then_inc(free, 1)

        def pack(eng, copy, t, h, quadrants, done):
            eng.wait_ge(s_gram, ROUNDS * t + h + 1)
            for j in quadrants:
                for k in range(SPG):
                    n = min(GB, F - 1 - GB * k)
                    m = GROUPS_PER_ROUND
                    at = (F - 1) * j + GB * k
                    src = ps_gram[Q * j:Q * j + Q, h % 2, :, at:at + n]
                    last = copy(pairs[Q * k:Q * k + Q, 0:n, t, j, m * h:m * h + m],
                                src.rearrange("f m g -> f g m"))
            last.then_inc(done, 1)

        @block.scalar
        def _(act):
            def copy(dst, src):
                return act.activation(dst, src, ACT.Copy)

            def zero_pads(t):
                act.activation(feat[:, t:t + 2, :, F:Q].rearrange("d t p f -> d (t p) f"),
                               zero[:, :].unsqueeze(2).to_broadcast([D, 2 * P, Q - F]), ACT.Copy)\
                   .then_inc(s_pad, 1)

            def ids_out(i):
                act.wait_ge(s_bc, i + 1)
                if i >= SPLITS:
                    act.wait_ge(s_oh, CD * (i - SPLITS + 1))
                copy(ids_all[:, i % SPLITS, :], ps_l[i % 2][:, :]).then_inc(s_lfree[i % 2], 1)

            def split_hi(i):
                act.wait_ge(s_raw[i % RAWS], 16 * (i // RAWS + 1))
                if i >= SPLITS:
                    act.wait_ge(s_x, use_of[("look", i - SPLITS)] + 1)
                copy(table_hi[:, i % SPLITS, :], table[:, i % RAWS, :]).then_inc(s_hi, 1)

            def split_hi_first(half, landed):
                act.wait_ge(landed, 16)
                at = slice(half * HALF, half * HALF + HALF)
                copy(table_hi[:, 0, at], table[:, 0, at]).then_inc(s_hi, 1)

            def compare_ids(i):
                b = i % SPLITS
                if i == 0:
                    act.wait_ge(s_consts, 1)
                if i >= SPLITS:
                    act.wait_ge(s_x, use_of[("look", i - SPLITS)] + 1)
                act.wait_ge(s_lfree[i % 2], i // 2 + 1)
                if i:
                    act.wait_ge(s_oh_act, i)
                act.activation(far[:, :], ids_all[0:RP, b, :], ACT.Abs, bias=minus_row[0:RP, :])\
                   .then_inc(s_far, 1)
                act.wait_ge(s_far, i + 1)
                act.activation(one_hot[:, b, CH - 1, :], far[:, :], ACT.Relu, bias=one[0:RP, :], scale=-1.0)\
                   .then_inc(s_oh_act, 1)

            def looked_out(i):
                use = ("look", i)
                act.wait_ge(s_x, use_of[use] + 1)
                dst = feat[:, :, :, ONE_HOT[i] + 1]
                copy(dst, ps_x[bank_of(use)][:, :].rearrange("d (t p) -> d t p", t=TILES))\
                    .then_inc(s_xfree[bank_of(use)], 1)

            act.wait_ge(s_zero, 1)
            zero_pads(0)
            act.wait_ge(s_ident, 1)
            copy(ident_r[:, :], ident[0:TABLES, 0:TABLES]).then_inc(s_idsT, 1)
            split_hi_first(0, s_first)
            act.wait_ge(s_set, 1)
            copy(ids_T[:, :], ps_gram[0:TABLES, 0, 0:TILES, :]).then_inc(s_idsT, 1)
            split_hi_first(1, s_raw[0])
            ids_out(0)
            compare_ids(0)
            split_hi(1)
            ids_out(1)
            act.wait_ge(s_x, 1)
            src = ps_x[0][:, :].rearrange("d (t p) -> d t p", t=TILES)
            for t in range(TILES):
                copy(dense_T[:, t, :].rearrange("d (j m) -> d j m", j=SPG),
                     src[:, t, :].rearrange("d (m j) -> d j m", j=SPG))
            copy(feat[:, :, :, 0], src).then_inc(s_xfree[0], 1)
            act.wait_ge(s_set, 2)
            copy(cols8[:, :], ps_gram[:, 1, 0, 0:C1 + 2 * C2]).then_inc(s_cols, 1)
            compare_ids(1)
            for i in range(len(ONE_HOT)):
                if i + 2 < len(ONE_HOT):
                    ids_out(i + 2)
                    split_hi(i + 2)
                looked_out(i)
                if i + 2 < len(ONE_HOT):
                    compare_ids(i + 2)
                if i:
                    evac_rows(act, copy, *early[i - 1][1:])
                if i == len(ONE_HOT) - 2:
                    zero_pads(2)
            act.wait_ge(s_cols, 1)
            def layer2_out(t):
                act.wait_ge(s_l[1], l_done(t, 2))
                in_order(act.activation, h2[:, 1, :], ps_l[1][:, 0:P], ACT.Relu, bias=cols8[:, C1 + 1:C1 + 2])\
                    .then_inc(s_lfree[1], 1)

            for t in range(TILES):
                rows_out(act, copy, between[t, 0])
                for h in range(ROUNDS):
                    pack(act, copy, t, h, (2, 3), s_pk_act)
                    rows_out(act, copy, between[t, h + 1])
                if t:
                    layer2_out(t - 1)
                    out_layer_out(act, copy, t - 1)
                rows_out(act, copy, between[t, IN_LAYER1] + between[t, IN_LAYER1 + 1])
                act.wait_ge(s_l[1], l_done(t, 1))
                for c in (2, 3):
                    if c == 3 and t == TILES - 1:
                        last.then_inc(s_lfree[1], 1)
                        act.wait_ge(s_tail, 1)
                    last = act.activation(h1[:, c, :], layer1_column(t, c), ACT.Relu, bias=cols8[:, c:c + 1])
                last.then_inc(s_lfree[1] if t < TILES - 1 else s_tail_out, 1)
            layer2_out(TILES - 1)
            out_layer_out(act, copy, TILES - 1)

        @block.vector
        def _(dve):
            def copy(dst, src):
                return dve.tensor_copy(dst, src)

            dve.memset(zero[:, :], 0.0).then_inc(s_zero, 1)
            half = GB // 2 + 1
            dve.memset(w_pairs[:, 0:half, :], 0.0)
            dve.wait_ge(s_ids, 16)
            copy(ids_f[:, :], ids[:, :]).then_inc(s_idsf, 1)
            dve.memset(w_pairs[:, half:GB, :], 0.0).then_inc(s_zero, 1)

            def split_lo(i):
                b = i % SPLITS
                dve.wait_ge(s_hi, i + 2)
                if i >= SPLITS:
                    dve.wait_ge(s_x, use_of[("look", i - SPLITS)] + 1)
                dve.tensor_tensor(table_lo[:, b, :], table[:, i % RAWS, :], table_hi[:, b, :].bitcast(fp32),
                                  ALU.subtract).then_inc(s_lo, 1)

            def split_lo_first(half):
                dve.wait_ge(s_hi, half + 1)
                at = slice(half * HALF, half * HALF + HALF)
                dve.tensor_tensor(table_lo[:, 0, at], table[:, 0, at], table_hi[:, 0, at].bitcast(fp32),
                                  ALU.subtract).then_inc(s_lo, 1)

            def compare_ids(i):
                b = i % SPLITS
                dve.wait_ge(s_lfree[i % 2], i // 2 + 1)
                if i >= SPLITS:
                    dve.wait_ge(s_x, use_of[("look", i - SPLITS)] + 1)
                for c in range(CD):
                    dve.tensor_scalar(one_hot[:, b, c, :], ids_all[0:RP, b, :], row_of[0:RP, c:c + 1], None,
                                      ALU.is_equal).then_inc(s_oh, 1)

            dve.memset(one[:, :], 1.0)
            dve.wait_ge(s_ident, 2)
            dve.tensor_scalar(minus_row[:, :], row_of[:, CH - 1:CH], -1.0, None, ALU.mult).then_inc(s_consts, 1)
            for i in range(len(ONE_HOT)):
                if i:
                    split_lo(i)
                else:
                    split_lo_first(0)
                    split_lo_first(1)
                compare_ids(i)
            dve.wait_ge(s_wd, 32)
            dve.tensor_tensor(w_dense[:, 0, :], w_dense[:, 0, :], w_dense[:, 1, :], ALU.add).then_inc(s_wds, 1)
            dve.wait_ge(s_cols, 1)

            def relu(dst, src, bias):
                return dve.tensor_scalar(dst, src, bias, 0.0, ALU.add, ALU.max)

            def layer2_out(t):
                dve.wait_ge(s_l[0], l_done(t, 2))
                in_order(relu, h2[:, 0, :], ps_l[0][:, 0:P], cols8[:, C1:C1 + 1]).then_inc(s_lfree[0], 1)

            for t in range(TILES):
                rows_out(dve, copy, between[t, 0])
                for h in range(ROUNDS):
                    pack(dve, copy, t, h, (0, 1), s_pk_dve)
                    rows_out(dve, copy, between[t, h + 1])
                if t:
                    layer2_out(t - 1)
                    out_layer_out(dve, copy, t - 1)
                rows_out(dve, copy, between[t, IN_LAYER1] + between[t, IN_LAYER1 + 1])
                dve.wait_ge(s_l[0], l_done(t, 1))
                for c in (0, 1):
                    last = relu(h1[:, c, :], layer1_column(t, c), cols8[:, c:c + 1])
                last.then_inc(s_lfree[0], 1)
            layer2_out(TILES - 1)
            out_layer_out(dve, copy, TILES - 1)

        @block.tensor
        def _(pe):
            def keep_warm(n):
                for _ in range(n):
                    pe.transpose(ps_l[1][:, 0:P], ident[:, :], ident[:, :])

            pe.wait_ge(s_ident, 1)
            keep_warm(8)
            pe.wait_ge(s_idsf, 1)
            for t in range(TILES):
                last = pe.transpose(ps_gram[0:TABLES, 0, t, :], ids_f[:, t * TABLES:t * TABLES + TABLES], ident[:, :])
            last.then_inc(s_set, 1)
            def broadcast_ids(i):
                if i == 0:
                    pe.wait_ge(s_idsT, 2)
                if i >= 2:
                    pe.wait_ge(s_lfree[i % 2], i // 2)
                tb = ONE_HOT[i]
                pe.matmul(ps_l[i % 2][:, :], ident_r[:, tb:tb + 1].to_broadcast([TABLES, P]), ids_T[:, :],
                          start=True, stop=True).then_inc(s_bc, 1)

            def lookup(i):
                b = i % SPLITS
                use = ("look", i)
                wait_bank(pe, use)
                pe.wait_ge(s_hi, i + 2)
                pe.wait_ge(s_lo, i + 2)
                for c in range(CH):
                    if c < CD:
                        pe.wait_ge(s_oh, CD * i + c + 1)
                    else:
                        pe.wait_ge(s_oh_act, i + 1)
                    pe.matmul(ps_x[bank_of(use)][:, :], table_hi[:, b, c * D:c * D + D], one_hot[:, b, c, :],
                              start=(c == 0), stop=False)
                    last = pe.matmul(ps_x[bank_of(use)][:, :], table_lo[:, b, c * D:c * D + D], one_hot[:, b, c, :],
                                     start=False, stop=(c == CH - 1))
                last.then_inc(s_x, 1)

            def transpose_rows(t, g):
                u = ("rows", t, g)
                bank, full, free, use = rows_bank(u)
                if u not in early:
                    wait_bank(pe, u)
                elif use >= 2:
                    pe.wait_ge(free, use - 1)
                elif use == 1:
                    pe.wait_ge(s_cols, 1)
                pe.wait_ge(s_rows[t][g], 16 * GROUPS[g][2])
                for n in range(GROUPS[g][2]):
                    last = pe.transpose(bank[:, n * P:n * P + P],
                                        rows[:, GROUP_AT[g] + n, t % ROW_BUFS, :], ident[:, :])
                last.then_inc(full, 1)

            def grams(t, h):
                r = ROUNDS * t + h
                if h == 0:
                    wait_feat(pe, t)
                    if t % 2 == 0:
                        pe.wait_ge(s_pad, t // 2 + 1)
                if r < 2:
                    pe.wait_ge(s_early_out, len(early) - (r == len(early) % 2))
                else:
                    pe.wait_ge(s_pk_act, r - 1)
                    pe.wait_ge(s_pk_dve, r - 1)
                for m in range(GROUPS_PER_ROUND):
                    at = (h * GROUPS_PER_ROUND + m) * SPG
                    samples = feat[:, t, at:at + SPG, :]
                    last = pe.matmul(ps_gram[:, h % 2, m, 0:SPG * (F - 1)], samples.rearrange("d s f -> d (s f)"),
                                     samples[:, :, 1:F], start=True, stop=True)
                last.then_inc(s_gram, 1)

            def layer1(t):
                if t == 0:
                    pe.wait_ge(s_wds, 1)
                    pe.wait_ge(s_w1, 16 * PAIR_LOADS)
                def column(c):
                    return layer1_column(t, c)

                def from_dense(c):
                    pe.matmul(column(c), w_dense[:, 0, c * P:c * P + P], dense_T[:, t, :], start=True, stop=False)

                def from_pairs(c):
                    for g in range(GB):
                        kp = P if GB * (SPG - 1) + g < F - 1 else P - Q
                        last = pe.matmul(column(c), w_pairs[0:kp, g, c * P:c * P + P],
                                         pairs[0:kp, g, t, :, :].rearrange("p j m -> p (j m)"),
                                         start=False, stop=(g == GB - 1))
                    return last

                pe.wait_ge(s_lfree[0], l_before(0, t, 1))
                from_dense(0)
                pe.wait_ge(s_pk_act, ROUNDS * (t + 1))
                pe.wait_ge(s_pk_dve, ROUNDS * (t + 1))
                from_pairs(0)
                from_dense(1)
                from_pairs(1).then_inc(s_l[0], 1)
                if t:
                    out_layer(t - 1)
                for u in between[t, IN_LAYER1]:
                    transpose_rows(*u[1:])
                pe.wait_ge(s_lfree[1], l_before(1, t, 1))
                for c in (2, 3):
                    if c == 3:
                        if t == TILES - 1:
                            last.then_inc(s_l[1], 1)
                        for u in between[t, IN_LAYER1 + 1]:
                            transpose_rows(*u[1:])
                    from_dense(c)
                    last = from_pairs(c)
                last.then_inc(s_l[1] if t < TILES - 1 else s_tail, 1)

            def layer2(t):
                if t == 0:
                    pe.wait_ge(s_w2, 16)
                for m in range(C2):
                    for c in range(C1):
                        if m == 0 and c % 2 == 0:
                            b = c // 2
                            pe.wait_ge(s_lfree[b], l_before(b, t, 2))
                        if m == 0 and c == C1 - 1 and t == TILES - 1:
                            pe.wait_ge(s_tail_out, 1)
                        last = pe.matmul(ps_l[m][:, 0:P], w2[:, c, m * P:m * P + P], h1[:, c, :],
                                         start=(c == 0), stop=(c == C1 - 1))
                    last.then_inc(s_l[m], 1)

            def out_layer(t):
                u = ("out", t)
                wait_bank(pe, u)
                pe.wait_ge(s_lfree[0], l_before(0, t, 2) + 1)
                pe.wait_ge(s_lfree[1], l_before(1, t, 2) + 1)
                for m in range(C2):
                    last = pe.matmul(ps_x[bank_of(u)][:, 0:1], h2[:, m, :], cols8[:, C1 + C2 + m:C1 + C2 + m + 1],
                                     start=(m == 0), stop=(m == C2 - 1))
                last.then_inc(s_x, 1)

            keep_warm(5)
            broadcast_ids(0)
            pe.wait_ge(s_dense, 16)
            for t in range(TILES):
                last = pe.transpose(ps_x[0][:, t * P:t * P + P], dense[:, t, :], ident[:, :])
            last.then_inc(s_x, 1)
            broadcast_ids(1)
            pe.wait_ge(s_small, 48)
            pe.transpose(ps_gram[:, 1, 0, 0:C1 + 2 * C2], rows8[:, :], ident[0:C1 + 2 * C2, 0:C1 + 2 * C2])\
              .then_inc(s_set, 1)
            for i in range(len(ONE_HOT)):
                if i + 2 < len(ONE_HOT):
                    broadcast_ids(i + 2)
                lookup(i)
                if i:
                    transpose_rows(*early[i - 1][1:])
            for t in range(TILES):
                for u in between[t, 0]:
                    transpose_rows(*u[1:])
                for h in range(ROUNDS):
                    grams(t, h)
                    for u in between[t, h + 1]:
                        transpose_rows(*u[1:])
                if t:
                    layer2(t - 1)
                layer1(t)
            layer2(TILES - 1)
            out_layer(TILES - 1)


_IN = (["r_dense_features", "ids"] + [f"tbl_{i}" for i in range(TABLES)]
       + ["W_top1", "b_top1", "W_top2", "b_top2", "W_top3"])


def kernel(**inputs):
    import numpy as _np
    import concourse.bacc as _bacc
    from concourse import mybir as _mybir
    from concourse.bass_utils import run_bass_kernel_spmd as _run

    nc = _bacc.Bacc("TRN2", target_bir_lowering=False, num_devices=1)
    arrays, args = {}, {}
    for name in _IN:
        a = _np.ascontiguousarray(inputs[name])
        arrays[f"in_{name}_dram"] = a
        args[name] = nc.dram_tensor(f"in_{name}_dram", a.shape, _mybir.dt.from_np(a.dtype),
                                    kind="ExternalInput").ap()
    out = nc.dram_tensor("out_0_dram", (BATCH, 1), _mybir.dt.float32, kind="ExternalOutput").ap()
    dlrm_tower(nc, args, out)
    r = _run(nc, [arrays], core_ids=[0])
    return r.results[0]["out_0_dram"]
```

```python
import concourse.bass as bass
from concourse import mybir
from contextlib import ExitStack

fp32 = mybir.dt.float32
fp32r = mybir.dt.float32r
int32 = mybir.dt.int32
ALU = mybir.AluOpType
ACT = mybir.ActivationFunctionType

P = 128
D = 128
TABLES = 26
F = TABLES + 1
TILES = 4
BATCH = TILES * P
ONE_HOT = [18, 20, 22, 23, 24, 25, 0]
SPREAD_ON_PE = 2
ROWS = 1000
CH = 8
CD = CH - 1
RP = ROWS // CH
GATHER = [i for i in range(TABLES) if i not in ONE_HOT]
NG = len(GATHER)
GROUPS = [(2, 1, 4), (6, 1, 4), (10, 1, 4), (14, 1, 4), (18, 2, 3)]
GROUP_AT = [sum(n for _, _, n in GROUPS[:g]) for g in range(len(GROUPS))]
assert [f + s * i for f, s, n in GROUPS for i in range(n)] == [i + 1 for i in GATHER]
Q = 32
SPG = 4
GB = 7
GROUPS_PER_ROUND = 8
ROUNDS = P // (SPG * GROUPS_PER_ROUND)
ROW_BUFS = 3
BETWEEN = [(1, 0, 0, 0, 2, 2), (0, 0, 1, 0, 1, 2), (0, 1, 0, 1, 1, 2), (0,) * 6]
N1, N2 = 512, 256
C1, C2 = N1 // P, N2 // P
KC = GB + 1
PAIRS = F * (F - 1) // 2
PAIR_LOADS = F - 1


def pair_row(f, g):
    return D + f * F - f * (f + 1) // 2 + g - f - 1


def load_pairs(sp, f, w_pairs, w_top1, loaded):
    k = f // GB
    r = pair_row(f, 1 + GB * k)
    sp.dma_start(w_pairs[Q * k + f:P:Q, :, :],
                 w_top1[r:r + GB * (SPG - k), :].rearrange("(k g) n -> k g n", g=GB)).then_inc(loaded, 16)


def dlrm_tower(nc, A, out):
    ctx = ExitStack()
    with ctx:
        def sb(name, shape, dt=fp32):
            return ctx.enter_context(nc.sbuf_tensor(name, shape, dt))

        def sem(name):
            return ctx.enter_context(nc.semaphore(name))

        RAWS, SPLITS = 3, 2
        HALF = CH * D // 2
        ids = sb("ids_i", [P, TILES * TABLES], int32)
        ids_f = sb("ids_f", [P, TILES * TABLES])
        ids_T = sb("ids_T", [TABLES, BATCH])
        ident = sb("ident", [P, P])
        row_of = sb("row_of", [P, CH])
        is_pair = sb("is_pair", [P, GB])
        zero = sb("zero", [P, 1])
        one = sb("one", [P, 1])
        minus_row = sb("minus_row", [P, 1])
        far = sb("far", [RP, BATCH])
        dense = sb("dense", [P, TILES, D])
        dense_T = sb("dense_T", [D, TILES, P])
        rows = sb("rows", [P, NG, ROW_BUFS, D])
        feat = sb("feat", [D, TILES, P, Q])
        table = sb("table", [RP, RAWS, CH * D])
        table_hi = sb("table_hi", [P, SPLITS, CH * D], fp32r)
        table_lo = sb("table_lo", [P, SPLITS, CH * D], fp32r)
        ids_dram = nc.dram_tensor("ids_dram", (TABLES, BATCH), fp32).ap()
        one_hot = sb("one_hot", [P, SPLITS, CH, BATCH], fp32r)
        pairs = sb("pairs", [P, GB, TILES, SPG, P // SPG])
        assert len(ONE_HOT) == GB
        ids_all = pairs[:, :, :, :, :].rearrange("p g t j m -> p g (t j m)")
        assert KC * P == CH * D and KC == CH and BATCH == N1 and SPLITS == 2
        w_hi, w_lo = one_hot[:, 1, :, :], one_hot[:, 0, :, :]
        x_hi = table_hi[:, :, :].rearrange("k b (c j m) -> k b c j m", c=KC, j=SPG)
        x_lo = table_lo[:, :, :].rearrange("k b (c j m) -> k b c j m", c=KC, j=SPG)
        w_pairs = sb("w_pairs", [P, GB, N1])
        w_dense = sb("w_dense", [P, 2, N1])
        w2 = sb("w2", [P, C1, N2])
        rows8 = sb("rows8", [C1 + 2 * C2, P])
        cols8 = sb("cols8", [P, C1 + 2 * C2])
        h1_rows = sb("h1_rows", [P, N1])
        h1 = sb("h1", [P, C1, P])
        h2 = sb("h2", [P, C2, P])
        y = sb("y", [P, TILES])

        ps_gram = ctx.enter_context(nc.psum_tensor("ps_gram", [P, 2, GROUPS_PER_ROUND, P], fp32))
        ps_x = [ctx.enter_context(nc.psum_tensor(f"ps_x{b}", [P, 512], fp32)) for b in range(2)]
        ps_l = [ctx.enter_context(nc.psum_tensor(f"ps_l{b}", [P, 512], fp32)) for b in range(2)]

        s_ids = sem("s_ids")
        s_small = sem("s_small")
        s_dense = sem("s_dense")
        s_w1 = sem("s_w1")
        s_wd = sem("s_wd")
        s_w2 = sem("s_w2")
        s_first = sem("s_first")
        s_raw = [sem(f"s_raw{b}") for b in range(RAWS)]
        s_rows = [[sem(f"s_rows{t}_{g}") for g in range(len(GROUPS))] for t in range(TILES)]
        s_out = sem("s_out")
        s_memz = sem("s_memz")
        s_mask = sem("s_mask")
        s_ident = sem("s_ident")
        s_zero = sem("s_zero")
        s_pad = sem("s_pad")
        s_idsf = sem("s_idsf")
        s_set = sem("s_set")
        s_idsT = sem("s_idsT")
        s_dense_out = sem("s_dense_out")
        s_cols = sem("s_cols")
        s_bc = sem("s_bc")
        s_ids_dram = sem("s_ids_dram")
        s_spread = [sem(f"s_spread{i}") for i in range(SPREAD_ON_PE, len(ONE_HOT))]
        s_hi = sem("s_hi")
        s_lo = sem("s_lo")
        s_oh = sem("s_oh")
        s_far = sem("s_far")
        s_oh_act = sem("s_oh_act")
        s_consts = sem("s_consts")
        s_x = sem("s_x")
        s_xfree = [sem(f"s_xfree{b}") for b in range(2)]
        s_early = sem("s_early")
        s_early_out = sem("s_early_out")
        s_wds = sem("s_wds")
        s_gram = sem("s_gram")
        s_pk_act = sem("s_pk_act")
        s_pk_dve = sem("s_pk_dve")
        s_ids_free = [sem(f"s_ids_free{b}") for b in range(2)]
        s_whi = sem("s_whi")
        s_wlo = sem("s_wlo")
        s_xhi = sem("s_xhi")
        s_xlo = sem("s_xlo")
        s_l1 = sem("s_l1")
        s_rows1 = sem("s_rows1")
        s_turned = [sem(f"s_turned{b}") for b in range(2)]
        s_h1 = [sem(f"s_h1{b}") for b in range(2)]
        s_l2 = [sem(f"s_l2{m}") for m in range(2)]
        s_h2 = [sem(f"s_h2{m}") for m in range(2)]

        AFTER_LAYER1 = ROUNDS + 1
        order = [("rows", t, g) for t in range(TILES) for g in range(len(GROUPS))]
        early = order[:len(ONE_HOT) - 1]
        between, at = {}, len(early)
        uses = [("look", i) for i in range(len(ONE_HOT))]
        for t in range(TILES):
            for step in range(ROUNDS + 2):
                n = BETWEEN[t][step]
                between[t, step] = order[at:at + n]
                at += n
                uses += between[t, step]
            if t:
                uses += [("out", t - 1)]
        uses += [("out", TILES - 1)]
        assert at == len(order)
        use_of = {u: n for n, u in enumerate(uses)}

        def bank_of(use):
            return use_of[use] % 2

        def wait_bank(eng, use):
            n = use_of[use]
            if n >= 2:
                eng.wait_ge(s_xfree[n % 2], n // 2)

        def wait_feat(eng, t):
            if t < 2:
                eng.wait_ge(s_early_out, len([u for u in early if u[1] <= t]))
            n = use_of.get(("rows", t, len(GROUPS) - 1), use_of[("look", len(ONE_HOT) - 1)])
            eng.wait_ge(s_xfree[n % 2], n // 2 + 1)
            eng.wait_ge(s_xfree[1 - n % 2], (n + 1) // 2)

        def rows_bank(u):
            if u in early:
                n = early.index(u)
                return ps_gram[:, n % 2, 0:4, :].rearrange("d f p -> d (f p)"), s_early, s_early_out, n
            return ps_x[bank_of(u)][:, :], s_x, s_xfree[bank_of(u)], use_of[u]

        def layer1_parts(t):
            if t < TILES - 1:
                return [(0, N1, ps_l[0][:, :])]
            return [(0, N1 // 2, ps_l[0][:, 0:N1 // 2]),
                    (N1 // 2, N1, ps_gram[:, 0, 0:2, :].rearrange("p a b -> p (a b)"))]

        def layer2_psum(t, m):
            return ps_gram[:, 1, 0, :] if (t, m) == (TILES - 1, 1) else ps_l[m][:, 0:P]

        def wait_ids_all(eng, i):
            if i < SPREAD_ON_PE:
                eng.wait_ge(s_ids_free[i], 1)
            else:
                eng.wait_ge(s_spread[i - SPREAD_ON_PE], 16)

        def feat_fields(t, f, step, n):
            return feat[:, t, :, f:f + step * (n - 1) + 1:step].rearrange("d p f -> d f p")

        block = ctx.enter_context(nc.Block())

        @block.sync
        def _(sp):
            def load_table(i):
                sp.dma_start(table[:, i % RAWS, :], A[f"tbl_{ONE_HOT[i]}"].rearrange("(p c) d -> p (c d)", c=CH))\
                  .then_inc(s_raw[i % RAWS], 16)

            sp.dma_start(ids[:, :], A["ids"].rearrange("(p t) f -> p (t f)", t=TILES)).then_inc(s_ids, 16)
            for half, landed in ((0, s_first), (1, s_raw[0])):
                sp.dma_start(table[:, 0, half * HALF:half * HALF + HALF],
                             A[f"tbl_{ONE_HOT[0]}"].rearrange("(p c) d -> p (c d)", c=CH)
                             [:, half * HALF:half * HALF + HALF]).then_inc(landed, 16)
            sp.dma_start(dense[:, :, :], A["r_dense_features"].rearrange("(p t) d -> p t d", t=TILES))\
              .then_inc(s_dense, 16)
            sp.dma_start(rows8[0:C1, :], A["b_top1"].rearrange("(c p) -> c p", p=P)).then_inc(s_small, 16)
            sp.dma_start(rows8[C1:C1 + C2, :], A["b_top2"].rearrange("(c p) -> c p", p=P)).then_inc(s_small, 16)
            sp.dma_start(rows8[C1 + C2:C1 + 2 * C2, :], A["W_top3"].rearrange("(c p) o -> c (p o)", p=P))\
              .then_inc(s_small, 16)
            for i in range(1, RAWS):
                load_table(i)
            sp.wait_ge(s_idsT, 1)
            sp.dma_start(ids_dram, ids_T[:, :]).then_inc(s_ids_dram, 16)
            for i in range(RAWS, len(ONE_HOT)):
                sp.wait_ge(s_lo, i - RAWS + 2)
                load_table(i)
                if i == RAWS:
                    sp.wait_ge(s_ids_dram, 16)
                first = SPREAD_ON_PE + 2 * (i - RAWS)
                for n in range(first, min(first + 2, len(ONE_HOT))):
                    sp.dma_start(ids_all[:, n, :], ids_dram[ONE_HOT[n]:ONE_HOT[n] + 1, :].to_broadcast([P, BATCH]))\
                      .then_inc(s_spread[n - SPREAD_ON_PE], 16)
                if i == RAWS:
                    sp.wait_ge(s_zero, 2)
                if i == len(ONE_HOT) - 1:
                    for half, r0 in enumerate((0, D + PAIRS)):
                        sp.dma_start(w_dense[:, half, :], A["W_top1"][r0:r0 + D, :]).then_inc(s_wd, 16)
                n = 3
                first = n * (i - RAWS)
                for f in range(first, first + n if i + 1 < len(ONE_HOT) else F - 1):
                    load_pairs(sp, f, w_pairs, A["W_top1"], s_w1)
            sp.dma_start(w2[:, :, :], A["W_top2"].rearrange("(c p) n -> p c n", p=P)).then_inc(s_w2, 16)
            for b in range(2):
                sp.wait_ge(s_xfree[b], len(range(b, len(uses), 2)))
            sp.dma_start(out.rearrange("(p t) c -> p (t c)", t=TILES), y[:, :]).then_inc(s_out, 16)
            sp.wait_ge(s_out, 16)

        @block.gpsimd
        def _(pool):
            pool.memset(ident[:, :], 0.0).then_inc(s_memz, 1)
            pool.wait_ge(s_memz, 1)
            pool.affine_select(out=ident[:, :], in_=ident[:, :], compare_op=ALU.not_equal, fill=1.0,
                               base=0, pattern=[[-1, P]], channel_multiplier=1).then_inc(s_ident, 1)
            pool.iota(row_of[:, :], pattern=[[1, CH]], base=0, channel_multiplier=CH,
                      allow_small_or_imprecise_dtypes=True).then_inc(s_ident, 1)
            pool.memset(is_pair[:, :], 1.0).then_inc(s_mask, 1)
            pool.wait_ge(s_mask, 1)
            for k in range(SPG):
                quadrant = is_pair[Q * k:Q * k + Q, :]
                pool.affine_select(out=quadrant, in_=quadrant, compare_op=ALU.is_gt, fill=0.0,
                                   base=1 + GB * k, pattern=[[1, GB]], channel_multiplier=-1).then_inc(s_mask, 1)
            pool.wait_ge(s_mask, 1 + SPG)
            pool.wait_ge(s_ids, 16)
            for t in range(TILES):
                if t >= ROW_BUFS:
                    _, full, _, use = rows_bank(("rows", t - ROW_BUFS, len(GROUPS) - 1))
                    pool.wait_ge(full, use + 1)
                for g, (_, _, n) in enumerate(GROUPS):
                    for at in range(GROUP_AT[g], GROUP_AT[g] + n):
                        col = t * TABLES + GATHER[at]
                        pool.indirect_dma_start(
                            rows[:, at, t % ROW_BUFS, :], None, A[f"tbl_{GATHER[at]}"],
                            bass.IndirectOffsetOnAxis(ap=ids[:, col:col + 1], axis=0),
                        ).then_inc(s_rows[t][g], 16)

        def read_by(u):
            return (nc.scalar, nc.vector)[bank_of(u)]

        def out_layer_out(eng, copy, t):
            u = ("out", t)
            if read_by(u) is eng:
                eng.wait_ge(s_x, use_of[u] + 1)
                copy(y[:, t:t + 1], ps_x[bank_of(u)][:, 0:1]).then_inc(s_xfree[bank_of(u)], 1)

        def in_order(op, dst, src, *args, **kw):
            return op(dst.rearrange("n (m j) -> n j m", j=SPG), src.rearrange("n (j m) -> n j m", j=SPG), *args, **kw)

        def rows_out(eng, copy, groups):
            for u in groups:
                if read_by(u) is eng:
                    evac_rows(eng, copy, *u[1:])

        def evac_rows(eng, copy, t, g):
            f, step, n = GROUPS[g]
            bank, full, free, use = rows_bank(("rows", t, g))
            eng.wait_ge(full, use + 1)
            copy(feat_fields(t, f, step, n), bank[:, 0:n * P].rearrange("d (f p) -> d f p", p=P)).then_inc(free, 1)

        half_tile = P // SPG // 2
        columns_of_part = (slice(0, half_tile), slice(half_tile, 2 * half_tile))

        def pack(eng, copy, t, h, quadrants, done):
            eng.wait_ge(s_gram, ROUNDS * t + h + 1)
            for j in quadrants:
                for k in range(SPG):
                    n = min(GB, F - 1 - GB * k)
                    m = GROUPS_PER_ROUND
                    at = (F - 1) * j + GB * k
                    src = ps_gram[Q * j:Q * j + Q, h % 2, :, at:at + n]
                    last = copy(pairs[Q * k:Q * k + Q, 0:n, t, j, m * h:m * h + m],
                                src.rearrange("f m g -> f g m"))
            last.then_inc(done, 1)

        @block.scalar
        def _(act):
            def copy(dst, src):
                return act.activation(dst, src, ACT.Copy)

            def zero_pads(t):
                act.activation(feat[:, t:t + 2, :, F:Q].rearrange("d t p f -> d (t p) f"),
                               zero[:, :].unsqueeze(2).to_broadcast([D, 2 * P, Q - F]), ACT.Copy)\
                   .then_inc(s_pad, 1)

            def ids_out(i):
                act.wait_ge(s_bc, i + 1)
                copy(ids_all[:, i, :], ps_l[i][:, :]).then_inc(s_ids_free[i], 1)

            def split_hi(i):
                act.wait_ge(s_raw[i % RAWS], 16 * (i // RAWS + 1))
                if i >= SPLITS:
                    act.wait_ge(s_x, use_of[("look", i - SPLITS)] + 1)
                copy(table_hi[0:RP, i % SPLITS, :], table[:, i % RAWS, :]).then_inc(s_hi, 1)

            def split_hi_first(half, landed):
                act.wait_ge(landed, 16)
                at = slice(half * HALF, half * HALF + HALF)
                copy(table_hi[0:RP, 0, at], table[:, 0, at]).then_inc(s_hi, 1)

            def compare_ids(i):
                if i == 0:
                    act.wait_ge(s_consts, 1)
                if i >= SPLITS:
                    act.wait_ge(s_x, use_of[("look", i - SPLITS)] + 1)
                wait_ids_all(act, i)
                if i:
                    act.wait_ge(s_oh_act, i)
                act.activation(far[:, :], ids_all[0:RP, i, :], ACT.Abs, bias=minus_row[0:RP, :])\
                   .then_inc(s_far, 1)
                act.wait_ge(s_far, i + 1)
                act.activation(one_hot[0:RP, i % SPLITS, CH - 1, :], far[:, :], ACT.Relu, bias=one[0:RP, :],
                               scale=-1.0).then_inc(s_oh_act, 1)

            def looked_out(i):
                use = ("look", i)
                act.wait_ge(s_x, use_of[use] + 1)
                dst = feat[:, :, :, ONE_HOT[i] + 1]
                copy(dst, ps_x[bank_of(use)][:, :].rearrange("d (t p) -> d t p", t=TILES))\
                    .then_inc(s_xfree[bank_of(use)], 1)

            def split_w(chunks):
                for c in chunks:
                    if c == 0:
                        act.wait_ge(s_mask, 1 + SPG)
                        act.wait_ge(s_w1, 16 * PAIR_LOADS)
                    if c == GB:
                        act.wait_ge(s_wds, 1)
                        copy(w_hi[:, c, :], w_dense[:, 0, :]).then_inc(s_whi, 1)
                    else:
                        act.activation(w_hi[:, c, :], w_pairs[:, c, :], ACT.Copy, scale=is_pair[:, c:c + 1])\
                           .then_inc(s_whi, 1)

            act.wait_ge(s_zero, 1)
            zero_pads(0)
            split_hi_first(0, s_first)
            ids_out(0)
            split_hi_first(1, s_raw[0])
            act.wait_ge(s_set, 1)
            copy(ids_T[:, :], ps_gram[0:TABLES, 0, 0:TILES, :]).then_inc(s_idsT, 1)
            compare_ids(0)
            ids_out(1)
            split_hi(1)
            compare_ids(1)
            for i in range(len(ONE_HOT)):
                if i + 2 < len(ONE_HOT):
                    split_hi(i + 2)
                looked_out(i)
                if i + 2 < len(ONE_HOT):
                    compare_ids(i + 2)
                if i:
                    evac_rows(act, copy, *early[i - 1][1:])
                if i == len(ONE_HOT) - 3:
                    act.wait_ge(s_set, 2)
                    for t in range(TILES):
                        copy(dense_T[:, t, :].rearrange("d (j m) -> d j m", j=SPG),
                             ps_gram[:, 0, 4 + t, :].rearrange("d (m j) -> d j m", j=SPG))
                    copy(feat[:, :, :, 0], ps_gram[:, 0, 4:4 + TILES, :]).then_inc(s_dense_out, 1)
                    act.wait_ge(s_set, 3)
                    copy(cols8[:, :], ps_gram[:, 1, 4, 0:C1 + 2 * C2]).then_inc(s_cols, 1)
                if i == len(ONE_HOT) - 2:
                    split_w(range(3))
            act.wait_ge(s_cols, 1)

            def split_x(t, part):
                b, m = t % 2, columns_of_part[part]
                packed = ROUNDS * t + ROUNDS // 2 * (part + 1)
                act.wait_ge(s_pk_act, packed)
                act.wait_ge(s_pk_dve, packed)
                if part == 0:
                    if t < 2:
                        act.wait_ge(s_x, use_of[("look", len(ONE_HOT) - 1)] + 1)
                    else:
                        act.wait_ge(s_l1, t - 1)
                    copy(x_hi[:, b, GB, :, :], dense_T[:, t, :].rearrange("d (j m) -> d j m", j=SPG))
                copy(x_hi[:, b, 0:GB, :, m], pairs[:, :, t, :, m]).then_inc(s_xhi, 1)

            def layer1_out(t):
                for n, (c0, c1, ps) in enumerate(layer1_parts(t)):
                    act.wait_ge(s_l1, t + 1 + n)
                    copy(h1_rows[:, c0:c1], ps).then_inc(s_rows1, 1)

            def h1_out(t):
                act.wait_ge(s_turned[1], t + 1)
                for c in (2, 3):
                    last = act.activation(h1[:, c, :], ps_l[1][:, (c - 2) * P:(c - 1) * P], ACT.Relu,
                                          bias=cols8[:, c:c + 1])
                last.then_inc(s_h1[1], 1)

            def layer2_out(t):
                act.wait_ge(s_l2[1], t + 1)
                in_order(act.activation, h2[:, 1, :], layer2_psum(t, 1), ACT.Relu, bias=cols8[:, C1 + 1:C1 + 2])\
                    .then_inc(s_h2[1], 1)

            for t in range(TILES):
                rows_out(act, copy, between[t, 0])
                if t == 0:
                    split_w((3, 4))
                for h in range(ROUNDS):
                    pack(act, copy, t, h, (2, 3), s_pk_act)
                    if h >= ROUNDS - 2:
                        split_x(t, h - (ROUNDS - 2))
                    if t == 0:
                        split_w(((5, 6), (), (7,), ())[h])
                    if h == ROUNDS - 1 and t:
                        layer2_out(t - 1)
                    rows_out(act, copy, between[t, h + 1])
                layer1_out(t)
                rows_out(act, copy, between[t, AFTER_LAYER1])
                if t:
                    out_layer_out(act, copy, t - 1)
                h1_out(t)
                if t == 0:
                    zero_pads(2)
            layer2_out(TILES - 1)
            out_layer_out(act, copy, TILES - 1)

        @block.vector
        def _(dve):
            def copy(dst, src):
                return dve.tensor_copy(dst, src)

            dve.memset(zero[:, :], 0.0).then_inc(s_zero, 1)
            half = GB // 2 + 1
            dve.memset(w_pairs[:, 0:half, :], 0.0)
            dve.wait_ge(s_ids, 16)
            copy(ids_f[:, :], ids[:, :]).then_inc(s_idsf, 1)
            dve.memset(w_pairs[:, half:GB, :], 0.0).then_inc(s_zero, 1)

            def split_lo(i):
                b = i % SPLITS
                dve.wait_ge(s_hi, i + 2)
                if i >= SPLITS:
                    dve.wait_ge(s_x, use_of[("look", i - SPLITS)] + 1)
                dve.tensor_tensor(table_lo[0:RP, b, :], table[:, i % RAWS, :], table_hi[0:RP, b, :].bitcast(fp32),
                                  ALU.subtract).then_inc(s_lo, 1)

            def split_lo_first(half):
                dve.wait_ge(s_hi, half + 1)
                at = slice(half * HALF, half * HALF + HALF)
                dve.tensor_tensor(table_lo[0:RP, 0, at], table[:, 0, at], table_hi[0:RP, 0, at].bitcast(fp32),
                                  ALU.subtract).then_inc(s_lo, 1)

            def compare_ids(i):
                b = i % SPLITS
                wait_ids_all(dve, i)
                if i >= SPLITS:
                    dve.wait_ge(s_x, use_of[("look", i - SPLITS)] + 1)
                for c in range(CD):
                    dve.tensor_scalar(one_hot[0:RP, b, c, :], ids_all[0:RP, i, :], row_of[0:RP, c:c + 1], None,
                                      ALU.is_equal).then_inc(s_oh, 1)

            dve.memset(one[:, :], 1.0)
            dve.wait_ge(s_ident, 2)
            dve.tensor_scalar(minus_row[:, :], row_of[:, CD:CH], -1.0, None, ALU.mult).then_inc(s_consts, 1)
            for i in range(len(ONE_HOT)):
                if i:
                    split_lo(i)
                else:
                    split_lo_first(0)
                    split_lo_first(1)
                compare_ids(i)
            dve.wait_ge(s_wd, 32)
            dve.tensor_tensor(w_dense[:, 0, :], w_dense[:, 0, :], w_dense[:, 1, :], ALU.add).then_inc(s_wds, 1)
            dve.wait_ge(s_cols, 1)

            def relu(dst, src, bias):
                return dve.tensor_scalar(dst, src, bias, 0.0, ALU.add, ALU.max)

            def split_w(chunks):
                for c in chunks:
                    dve.wait_ge(s_whi, c + 1)
                    hi = w_hi[:, c, :].bitcast(fp32)
                    if c < GB:
                        dve.scalar_tensor_tensor(w_lo[:, c, :], w_pairs[:, c, :], is_pair[:, c:c + 1], hi,
                                                 ALU.mult, ALU.subtract).then_inc(s_wlo, 1)
                    else:
                        dve.tensor_tensor(w_lo[:, c, :], w_dense[:, 0, :], hi, ALU.subtract).then_inc(s_wlo, 1)

            def split_x(t, part):
                b, m = t % 2, columns_of_part[part]
                dve.wait_ge(s_xhi, 2 * t + part + 1)
                if part == 0:
                    dve.tensor_tensor(x_lo[:, b, GB, :, :], dense_T[:, t, :].rearrange("d (j m) -> d j m", j=SPG),
                                      x_hi[:, b, GB, :, :].bitcast(fp32), ALU.subtract)
                dve.tensor_tensor(x_lo[:, b, 0:GB, :, m], pairs[:, :, t, :, m],
                                  x_hi[:, b, 0:GB, :, m].bitcast(fp32), ALU.subtract).then_inc(s_xlo, 1)

            def h1_out(t):
                dve.wait_ge(s_turned[0], t + 1)
                for c in (0, 1):
                    last = relu(h1[:, c, :], ps_l[0][:, c * P:c * P + P], cols8[:, c:c + 1])
                last.then_inc(s_h1[0], 1)

            def layer2_out(t):
                dve.wait_ge(s_l2[0], t + 1)
                in_order(relu, h2[:, 0, :], layer2_psum(t, 0), cols8[:, C1:C1 + 1]).then_inc(s_h2[0], 1)

            for t in range(TILES):
                rows_out(dve, copy, between[t, 0])
                if t == 0:
                    dve.wait_ge(s_x, use_of[("look", len(ONE_HOT) - 1)] + 1)
                    split_w((0, 1))
                for h in range(ROUNDS):
                    pack(dve, copy, t, h, (0, 1), s_pk_dve)
                    if h == ROUNDS - 1 and t:
                        layer2_out(t - 1)
                    if h == ROUNDS - 1:
                        for part in range(2):
                            split_x(t, part)
                    if t == 0:
                        split_w(((2,), (3,), (), (4, 5, 6, 7))[h])
                    rows_out(dve, copy, between[t, h + 1])
                rows_out(dve, copy, between[t, AFTER_LAYER1])
                h1_out(t)
                if t:
                    out_layer_out(dve, copy, t - 1)
            layer2_out(TILES - 1)
            out_layer_out(dve, copy, TILES - 1)

        @block.tensor
        def _(pe):
            def keep_warm(n):
                for _ in range(n):
                    pe.transpose(ps_l[1][:, 0:P], ident[:, :], ident[:, :])

            pe.wait_ge(s_ident, 1)
            keep_warm(8)
            pe.wait_ge(s_idsf, 1)

            def spread_ids(i):
                tb = ONE_HOT[i]
                for t in range(TILES):
                    last = pe.transpose(ps_l[i][:, t * P:t * P + P],
                                        ids_f[:, t * TABLES + tb:t * TABLES + tb + 1].to_broadcast([P, P]),
                                        ident[:, :])
                last.then_inc(s_bc, 1)

            def lookup(i):
                b = i % SPLITS
                use = ("look", i)
                wait_bank(pe, use)
                pe.wait_ge(s_hi, i + 2)
                pe.wait_ge(s_lo, i + 2)
                for c in range(CH):
                    if c < CD:
                        pe.wait_ge(s_oh, CD * i + c + 1)
                    else:
                        pe.wait_ge(s_oh_act, i + 1)
                    pe.matmul(ps_x[bank_of(use)][:, :], table_hi[0:RP, b, c * D:c * D + D], one_hot[0:RP, b, c, :],
                              start=(c == 0), stop=False)
                    last = pe.matmul(ps_x[bank_of(use)][:, :], table_lo[0:RP, b, c * D:c * D + D],
                                     one_hot[0:RP, b, c, :], start=False, stop=(c == CH - 1))
                last.then_inc(s_x, 1)

            def transpose_rows(t, g):
                u = ("rows", t, g)
                bank, full, free, use = rows_bank(u)
                if u not in early:
                    wait_bank(pe, u)
                elif use >= 2:
                    pe.wait_ge(free, use - 1)
                pe.wait_ge(s_rows[t][g], 16 * GROUPS[g][2])
                for n in range(GROUPS[g][2]):
                    last = pe.transpose(bank[:, n * P:n * P + P],
                                        rows[:, GROUP_AT[g] + n, t % ROW_BUFS, :], ident[:, :])
                last.then_inc(full, 1)

            def grams(t, h):
                r = ROUNDS * t + h
                if h == 0:
                    wait_feat(pe, t)
                    pe.wait_ge(s_dense_out, 1)
                    if t % 2 == 0:
                        pe.wait_ge(s_pad, t // 2 + 1)
                if r < 2:
                    pe.wait_ge(s_early_out, len(early) - (r == len(early) % 2))
                else:
                    pe.wait_ge(s_pk_act, r - 1)
                    pe.wait_ge(s_pk_dve, r - 1)
                for m in range(GROUPS_PER_ROUND):
                    at = (h * GROUPS_PER_ROUND + m) * SPG
                    samples = feat[:, t, at:at + SPG, :]
                    last = pe.matmul(ps_gram[:, h % 2, m, 0:SPG * (F - 1)], samples.rearrange("d s f -> d (s f)"),
                                     samples[:, :, 1:F], start=True, stop=True)
                last.then_inc(s_gram, 1)

            def layer1(t):
                if t:
                    pe.wait_ge(s_h2[0], t)
                else:
                    pe.wait_ge(s_ids_free[0], 1)
                parts = layer1_parts(t)
                terms = [(x, w, c) for x, w in ((x_hi, w_hi), (x_lo, w_hi), (x_hi, w_lo)) for c in range(KC)]
                ahead = [(x_hi, w_hi, GB), (x_hi, w_lo, GB)] if t else [(x_hi, w_hi, GB)]
                terms = [term for term in terms if term not in ahead]

                def product(part, term, start=False, stop=False):
                    (c0, c1, ps), (x, w, c) = part, term
                    if t == 0:
                        pe.wait_ge(s_wlo if w is w_lo else s_whi, c + 1)
                    kp = P - Q if F - 1 - GB * (SPG - 1) <= c < GB else P
                    return pe.matmul(ps, x[0:kp, t % 2, c, :, :].rearrange("k j m -> k (j m)"), w[0:kp, c, c0:c1],
                                     start=start, stop=stop)

                pe.wait_ge(s_xhi, 2 * t + 1)
                for n, part in enumerate(parts):
                    if n:
                        pe.wait_ge(s_pk_act, ROUNDS * (t + 1) - 1)
                        pe.wait_ge(s_pk_dve, ROUNDS * (t + 1) - 1)
                    for term in ahead:
                        product(part, term, start=(term is ahead[0]))
                pe.wait_ge(s_xhi, 2 * t + 2)
                for n, part in enumerate(parts):
                    for k, term in enumerate(terms):
                        if k == KC - 1:
                            pe.wait_ge(s_xlo, 2 * t + 2)
                            if n == 1:
                                turn_layer1(t, 0)
                        last = product(part, term, stop=(k == len(terms) - 1))
                    last.then_inc(s_l1, 1)

            def turn_layer1(t, b):
                pe.wait_ge(s_rows1, t + 1 + (b if t == TILES - 1 else 0))
                if b and t:
                    pe.wait_ge(s_h2[1], t)
                elif b:
                    pe.wait_ge(s_ids_free[1], 1)
                for c in range(2):
                    last = pe.transpose(ps_l[b][:, c * P:c * P + P], h1_rows[:, (2 * b + c) * P:(2 * b + c + 1) * P],
                                        ident[:, :])
                last.then_inc(s_turned[b], 1)

            def layer2(t, m, columns=range(C1)):
                if t == 0 and m == 0:
                    pe.wait_ge(s_w2, 16)
                for c in columns:
                    if m == 0 and c % 2 == 0:
                        pe.wait_ge(s_h1[c // 2], t + 1)
                    last = pe.matmul(layer2_psum(t, m), w2[:, c, m * P:m * P + P], h1[:, c, :],
                                     start=(c == 0), stop=(c == C1 - 1))
                if c == C1 - 1:
                    last.then_inc(s_l2[m], 1)

            def out_layer(t):
                u = ("out", t)
                wait_bank(pe, u)
                for m in range(C2):
                    pe.wait_ge(s_h2[m], t + 1)
                    last = pe.matmul(ps_x[bank_of(u)][:, 0:1], h2[:, m, :], cols8[:, C1 + C2 + m:C1 + C2 + m + 1],
                                     start=(m == 0), stop=(m == C2 - 1))
                last.then_inc(s_x, 1)

            spread_ids(0)
            for t in range(TILES):
                last = pe.transpose(ps_gram[0:TABLES, 0, t, :], ids_f[:, t * TABLES:t * TABLES + TABLES], ident[:, :])
            last.then_inc(s_set, 1)
            spread_ids(1)
            pe.wait_ge(s_dense, 16)
            for t in range(TILES):
                last = pe.transpose(ps_gram[:, 0, 4 + t, :], dense[:, t, :], ident[:, :])
            last.then_inc(s_set, 1)
            pe.wait_ge(s_small, 48)
            pe.transpose(ps_gram[:, 1, 4, 0:C1 + 2 * C2], rows8[:, :], ident[0:C1 + 2 * C2, 0:C1 + 2 * C2])\
              .then_inc(s_set, 1)
            for i in range(len(ONE_HOT)):
                lookup(i)
                if i:
                    transpose_rows(*early[i - 1][1:])
            for t in range(TILES):
                for u in between[t, 0]:
                    transpose_rows(*u[1:])
                for h in range(ROUNDS):
                    grams(t, h)
                    if h == ROUNDS - 1 and t:
                        for m in range(C2):
                            layer2(t - 1, m)
                    for u in between[t, h + 1]:
                        transpose_rows(*u[1:])
                layer1(t)
                for u in between[t, AFTER_LAYER1]:
                    transpose_rows(*u[1:])
                if t < TILES - 1:
                    turn_layer1(t, 0)
                if t:
                    out_layer(t - 1)
                turn_layer1(t, 1)
            for columns in ((0, 1), (2, 3)):
                for m in range(C2):
                    layer2(TILES - 1, m, columns)
            out_layer(TILES - 1)


_IN = (["r_dense_features", "ids"] + [f"tbl_{i}" for i in range(TABLES)]
       + ["W_top1", "b_top1", "W_top2", "b_top2", "W_top3"])


def kernel(**inputs):
    import numpy as _np
    import concourse.bacc as _bacc
    from concourse import mybir as _mybir
    from concourse.bass_utils import run_bass_kernel_spmd as _run

    nc = _bacc.Bacc("TRN2", target_bir_lowering=False, num_devices=1)
    arrays, args = {}, {}
    for name in _IN:
        a = _np.ascontiguousarray(inputs[name])
        arrays[f"in_{name}_dram"] = a
        args[name] = nc.dram_tensor(f"in_{name}_dram", a.shape, _mybir.dt.from_np(a.dtype),
                                    kind="ExternalInput").ap()
    out = nc.dram_tensor("out_0_dram", (BATCH, 1), _mybir.dt.float32, kind="ExternalOutput").ap()
    dlrm_tower(nc, args, out)
    r = _run(nc, [arrays], core_ids=[0])
    return r.results[0]["out_0_dram"]
```
